# Optimizing a Trainium2 kernel written in Bass

```python
import numpy as np
import jax
import jax.numpy as jnp

def _softmax(x, axis=-1):
    return jax.nn.softmax(x, axis=axis)

def _gelu(x):
    return jax.nn.gelu(x, approximate=True)

def _silu(x):
    return jax.nn.silu(x)

def _sigmoid(x):
    return jax.nn.sigmoid(x)

def _layernorm(x, axis=-1, eps=1e-05):
    m = jnp.mean(x, axis=axis, keepdims=True)
    v = jnp.var(x, axis=axis, keepdims=True)
    return (x - m) / jnp.sqrt(v + eps)

def _scatter_add(tgt, idx, src, axis=0):
    return tgt.at[idx].add(src)

def _segment_sum(src, seg, n):
    return jax.ops.segment_sum(src, seg, n)
kernel_name = 'mk_gnn_resnorm_d1_gnn_r32_c02805'

def setup_inputs(seed: int=0):
    np.random.seed(seed)
    _w = jnp.asarray

    def _rec_inputs():
        import jax
        import jax.numpy as jnp
        _gk = jax.random.key(seed)
        x = -0.0005121 + 1.001 * jax.random.normal(jax.random.fold_in(_gk, 1), (50000, 64), jnp.float32)
        src = jax.random.randint(jax.random.fold_in(_gk, 2), (50000,), 0, 50000, jnp.int32)
        dst = jnp.minimum((50000 * jax.random.uniform(jax.random.fold_in(_gk, 3), (50000,)) ** 2.0).astype(jnp.int32), 49999)
        _o = jnp.argsort(dst, stable=True)
        src = src[_o]
        dst = dst[_o]
        edge_attr_64 = 0.000189758 + 1.00013 * jax.random.normal(jax.random.fold_in(_gk, 11), (50000, 64), jnp.float32)
        return (x, src, dst, edge_attr_64)
    x, src, dst, edge_attr_64 = _rec_inputs()

    def _L0_gnn_setup():
        import jax, jax.numpy as jnp
        import numpy as np
        N = 50000
        E = 25000
        D_IN = 64
        D_HID = 128
        EPS = 1e-07
        LN_EPS = 1e-05

        def _layer_norm(h, g, b):
            mu = jnp.mean(h, axis=-1, keepdims=True)
            var = jnp.mean((h - mu) ** 2, axis=-1, keepdims=True)
            return (h - mu) * jax.lax.rsqrt(var + LN_EPS) * g + b
        key = jax.random.key(seed)
        ks = jax.random.split(key, 10)
        x = jax.random.normal(ks[0], (N, D_IN), dtype=jnp.float32)
        edge_index = jax.random.randint(ks[1], (2, E), 0, N, dtype=jnp.int32)
        edge_attr = jax.random.normal(ks[2], (E, D_IN), dtype=jnp.float32)
        s1 = 1.0 / np.sqrt(D_IN)
        s2 = 1.0 / np.sqrt(D_HID)
        W1 = jax.random.uniform(ks[3], (D_HID, D_IN), jnp.float32, -s1, s1)
        b1 = jax.random.uniform(ks[4], (D_HID,), jnp.float32, -s1, s1)
        g1 = jnp.ones((D_HID,), jnp.float32)
        be1 = jnp.zeros((D_HID,), jnp.float32)
        W2 = jax.random.uniform(ks[5], (D_IN, D_HID), jnp.float32, -s2, s2)
        b2 = jax.random.uniform(ks[6], (D_IN,), jnp.float32, -s2, s2)
        return {'x': x, 'edge_index': edge_index, 'edge_attr': edge_attr, 'W1': W1, 'b1': b1, 'g1': g1, 'be1': be1, 'W2': W2, 'b2': b2}
    _L0_gnn_all = _L0_gnn_setup()
    _L0_gnn_in = {k: v for k, v in _L0_gnn_all.items() if k in ('W1', 'b1', 'g1', 'be1', 'W2', 'b2')}
    del _L0_gnn_all
    return {'x': x, 'src': src, 'dst': dst, 'edge_attr_64': edge_attr_64, 'L0_gnn_W1': _L0_gnn_in['W1'], 'L0_gnn_b1': _L0_gnn_in['b1'], 'L0_gnn_g1': _L0_gnn_in['g1'], 'L0_gnn_be1': _L0_gnn_in['be1'], 'L0_gnn_W2': _L0_gnn_in['W2'], 'L0_gnn_b2': _L0_gnn_in['b2']}

def reference(x, src, dst, edge_attr_64, L0_gnn_W1, L0_gnn_b1, L0_gnn_g1, L0_gnn_be1, L0_gnn_W2, L0_gnn_b2):
    import jax
    import jax.numpy as jnp

    def _L0_gnn_ref(x, edge_index, edge_attr, W1, b1, g1, be1, W2, b2):
        import jax, jax.numpy as jnp
        import numpy as np
        N = 50000
        E = 25000
        D_IN = 64
        D_HID = 128
        EPS = 1e-07
        LN_EPS = 1e-05

        def _layer_norm(h, g, b):
            mu = jnp.mean(h, axis=-1, keepdims=True)
            var = jnp.mean((h - mu) ** 2, axis=-1, keepdims=True)
            return (h - mu) * jax.lax.rsqrt(var + LN_EPS) * g + b
        src = edge_index[0]
        dst = edge_index[1]
        msg = jax.nn.relu(x[src] + edge_attr) + EPS
        m = jax.ops.segment_max(msg, dst, num_segments=N)
        m = jnp.where(jnp.isfinite(m), m, 0.0)
        e = jnp.exp(msg - m[dst])
        denom = jax.ops.segment_sum(e, dst, num_segments=N)
        alpha = e / denom[dst]
        agg = jax.ops.segment_sum(alpha * msg, dst, num_segments=N)
        out = agg + x
        h = out @ W1.T + b1
        h = jax.nn.relu(_layer_norm(h, g1, be1))
        return h @ W2.T + b2
    edge_index = jnp.stack([src, dst])
    x = _layernorm(x + _L0_gnn_ref(x, edge_index, edge_attr_64, L0_gnn_W1, L0_gnn_b1, L0_gnn_g1, L0_gnn_be1, L0_gnn_W2, L0_gnn_b2), axis=-1)
    return x

_drawn_inputs = setup_inputs


def setup_inputs(seed=0):
    import zlib

    import numpy as np

    out = dict(_drawn_inputs(seed))
    spreads = {'L0_gnn_g1': (1.0, 0.2), 'L0_gnn_be1': (0.0, 0.1)}
    factors = {}
    for name, (base, spread) in spreads.items():
        noise = np.random.default_rng([zlib.crc32(name.encode()), seed]).standard_normal(out[name].shape)
        drawn = base * np.exp(spread * noise) if base else spread * noise
        out[name] = jnp.asarray(drawn.astype(out[name].dtype))
    for name, factor in factors.items():
        out[name] = (out[name] * factor).astype(out[name].dtype)
    return out
```

```python
from contextlib import ExitStack

import concourse.bass as bass
from concourse import mybir


P = 128
C = 64
G = 4
GROUP = P * G
EPS = 1e-07
LN_EPS = 1e-05
NEVER = 1e30

ALU = mybir.AluOpType
ACT = mybir.ActivationFunctionType
F32 = mybir.dt.float32
BF16 = mybir.dt.bfloat16
I32 = mybir.dt.int32
AX_X = mybir.AxisListType.X


class Step:

    def __init__(self, turn, place, ring):
        self.turn = turn + place // ring
        self.slot = place % ring
        self.j = self.turn * ring + self.slot
        self.known = isinstance(turn, int)


class Slot:

    def __init__(self, turn, place, ring, steps):
        self.turn, self.place, self.ring, self.steps = turn, place, ring, steps

    def step(self, off):
        s = Step(self.turn, self.place + off, self.ring)
        if s.known and not 0 <= s.j < self.steps:
            return None
        return s


def pipeline(engine, body, steps, ring, before, after):
    lo = -(-(after + 2) // ring)
    hi = (steps - before - 1) // ring
    for i in range(-before, lo * ring):
        body(Slot(i // ring, i % ring, ring, steps))
    with engine.Fori(lo, hi) as turn:
        for place in range(ring):
            body(Slot(turn, place, ring, steps))
    for i in range(hi * ring, steps + after):
        body(Slot(i // ring, i % ring, ring, steps))


def wait(engine, sem, n):
    if isinstance(n, int) and n <= 0:
        return
    engine.wait_ge(sem, n)


def gnn_resnorm(nc, x, src, dst, edge_attr, W1, b1, g1, be1, W2, b2, out):
    N = x.shape[0]
    E = src.shape[0]
    F = W1.shape[0]
    assert x.shape[1] == C and F == P
    HALF = -(-E // (2 * GROUP)) * GROUP
    NI = HALF // GROUP
    TILES = HALF // P
    TG = TILES // 2
    NB = -(-N // GROUP)
    NC = NB * G
    assert TG <= P and NC % 2 == 0 and NC // 2 <= 256 and NC <= 512 and N < 65535
    ZERO_ROW = 2 * HALF
    SPARE_ROW = 2 * HALF + 1
    MID = HALF
    tail_nodes = (N - (NB - 1) * GROUP) // G
    assert (N - (NB - 1) * GROUP) % G == 0

    mask_dram = nc.dram_tensor("mask_dram", (4, HALF), BF16, kind="Internal").ap()
    seg_rows = nc.dram_tensor("seg_rows", (2 * HALF + 2, C), F32, kind="Internal").ap()

    with ExitStack() as ctx:
        def sb(name, shape, dt=F32):
            return ctx.enter_context(nc.sbuf_tensor(name, shape, dt))

        def sem(name):
            return ctx.enter_context(nc.semaphore(name))

        psum = ctx.enter_context(nc.psum_tensor("psum", [P, 8, 512], F32))

        ramp = sb("ramp", [P, P])
        ident = sb("ident", [P, P])
        minus_ident = sb("minus_ident", [P, P])
        center = sb("center", [P, P])
        mean_w = sb("mean_w", [P, P])
        ones = sb("ones", [P, P])
        before_w = sb("before_w", [P, P])
        node_ramp = sb("node_ramp", [P, P])
        col_ramp = sb("col_ramp", [P, NC])
        node_ids = sb("node_ids", [P, P], BF16)
        col_ids = sb("col_ids", [P, NC], BF16)
        raw = sb("raw", [P, 3, 4, P], I32)
        rawf = sb("rawf", [P, 3, 4, P])
        src_idx = sb("src_idx", [P, TILES, 2], I32)
        dst_f = sb("dst_f", [P, TILES, 2])
        dst_i = sb("dst_i", [P, TILES, 2], I32)
        in_run = sb("in_run", [P, TILES])
        int_a = sb("int_a", [P, TILES, 2], I32)
        dst_p = sb("dst_p", [P, TILES, 2])
        dst_c = sb("dst_c", [P, TILES, 2])
        same_rows = sb("same_rows", [P, 2, 4, P], BF16)
        masks = sb("masks", [4, HALF], BF16)
        pick = sb("pick", [4, 2, P], BF16)
        mid_i = sb("mid_i", [P, 2], I32)
        mid_f = sb("mid_f", [P, 2])
        mid_cnt = sb("mid_cnt", [P, 4])
        mid_int = sb("mid_int", [P, 4], I32)
        w1_in = sb("w1_in", [P, 2, C])
        w2_in = sb("w2_in", [C, P])
        vecs = sb("vecs", [P, 3])
        w1_t = sb("w1_t", [P, P])
        w2_t = sb("w2_t", [P, C])
        b1_c = sb("b1_c", [P, 1])
        b2_row = sb("b2_row", [1, G, C])
        eps_col = sb("eps_col", [P, 2])
        zero_row = sb("zero_row", [2, C])

        src_slot = sb("src_slot", [P, 2, 2 * G], I32)
        x_src = sb("x_src", [P, 2, G, 2, C])
        e_sum = sb("e_sum", [P, 2, G, 2, C])
        same_bc = sb("same_bc", [P, 2, GROUP])
        state = sb("state", [P, 2, 3, GROUP + 1])
        below = sb("below", [P, 2, GROUP])
        e_exp = sb("e_exp", [P, 2, GROUP])
        c_exp = sb("c_exp", [P, 2, GROUP])
        e_msg = sb("e_msg", [P, 2, GROUP])
        log_d = sb("log_d", [P, 2, GROUP])
        quot = sb("quot", [P, 2, GROUP])
        row_out = sb("row_out", [P, 2, G, 2, C])
        hot_p = sb("hot_p", [P, 2, 2 * G, P], BF16)
        hot_c = sb("hot_c", [P, 2, 2 * G, NC], BF16)
        snap = sb("snap", [P, NI, 3])
        mrg = sb("mrg", [P, 16])

        count = sb("count", [P, NB, G])
        upto = sb("upto", [P, NB, G])
        block_n = sb("block_n", [P, NB])
        block_end = sb("block_end", [P, NB])
        block_0 = sb("block_0", [P, NB])
        some = sb("some", [P, NB, G])
        last_edge = sb("last_edge", [P, NB, G], I32)
        last_slot = sb("last_slot", [P, 4, G], I32)
        agg = sb("agg", [P, 4, G, C])
        x_in = sb("x_in", [P, 4, G, C])
        o_sum = sb("o_sum", [P, 4, G, C])
        o_t = sb("o_t", [P, 2, 2, P])
        sq = sb("sq", [P, 2, 2, 2 * P])
        inv = sb("inv", [P, 2, 2, 2 * P])
        h_n = sb("h_n", [P, 2, 2, 2, P])
        z = sb("z", [P, 4, G, C])
        z_sq = sb("z_sq", [P, 2, G, C])
        z_sum = sb("z_sum", [P, 2, G])
        z_var = sb("z_var", [P, 2, G])
        z_log = sb("z_log", [P, 2, G])
        z_inv = sb("z_inv", [P, 2, G])
        res = sb("res", [P, 4, G, C])

        pads_set = sem("pads_set")
        ramps_made = sem("ramps_made")
        loaded = sem("loaded")
        zero_set = sem("zero_set")
        prep = sem("prep")
        consts_made = sem("consts_made")
        masks_made = sem("masks_made")
        masks_out = sem("masks_out")
        masks_here = sem("masks_here")
        idx_turned = sem("idx_turned")
        idx_made = sem("idx_made")
        w_turned = sem("w_turned")
        w_made = sem("w_made")
        mid_counted = sem("mid_counted")
        mid_made = sem("mid_made")
        src_here = [sem(f"src_here{i}") for i in range(2)]
        attr_here = [sem(f"attr_here{i}") for i in range(2)]
        gathered = [sem(f"gathered{i}") for i in range(2)]
        gathers_open = sem("gathers_open")
        summed = sem("summed")
        turned = sem("turned")
        same_spread = sem("same_spread")
        same_copied = sem("same_copied")
        maxed = sem("maxed")
        carried = sem("carried")
        drop_made = sem("drop_made")
        below_made = sem("below_made")
        c_made = sem("c_made")
        e_made = sem("e_made")
        weighed = sem("weighed")
        d_made = sem("d_made")
        a_made = sem("a_made")
        snapped = sem("snapped")
        log_made = sem("log_made")
        inv_made = sem("inv_made")
        divided = sem("divided")
        turned_back = sem("turned_back")
        rows_made = sem("rows_made")
        rows_stored = [sem(f"rows_stored{i}") for i in range(2)]
        hot_made = sem("hot_made")
        counted = sem("counted")
        m_dve = sem("m_dve")
        m_pe = sem("m_pe")
        m_act = sem("m_act")
        merged_stored = sem("merged_stored")
        p_dve = sem("p_dve")
        p_pe = sem("p_pe")
        last_here = [sem(f"last_here{i}") for i in range(4)]
        x_here = [sem(f"x_here{i}") for i in range(4)]
        agg_here = [sem(f"agg_here{i}") for i in range(4)]
        o_summed = sem("o_summed")
        o_turned = sem("o_turned")
        o_copied = sem("o_copied")
        h_made = sem("h_made")
        sq_made = sem("sq_made")
        var_made = sem("var_made")
        hlog_made = sem("hlog_made")
        hinv_made = sem("hinv_made")
        h_scaled = sem("h_scaled")
        h_relu = sem("h_relu")
        y_made = sem("y_made")
        z_made = sem("z_made")
        z_summed = sem("z_summed")
        z_centered = sem("z_centered")
        z_squared = sem("z_squared")
        zvar_made = sem("zvar_made")
        zlog_made = sem("zlog_made")
        zinv_made = sem("zinv_made")
        normed = sem("normed")
        out_stored = [sem(f"out_stored{i}") for i in range(4)]

        idx_ps = psum[:, 0:2, 0:4 * TG].rearrange("p a (g t) -> p a g t", g=4)
        w_ps = psum[:, 3, :]
        msg_ps = psum[:, 0:2, :]
        same_ps = psum[:, 2, :]
        drop_ps = psum[:, 3:5, :]
        back_ps = psum[:, 5, :]
        count_ps = psum[:, 6, 0:NC]
        small_ps = psum[:, 7, :]
        ot_ps = psum[:, 0, 0:2 * P]
        h_ps = psum[:, 1:5, 0:2 * P].rearrange("p (s r) n -> p s r n", s=2)
        var_ps = psum[:, 5, :]
        y_ps = psum[:, 6:8, 0:G * C]

        def edge_rows(table, half, j):
            return table[bass.ds(j * GROUP + half * HALF, GROUP), :].rearrange("(k p) c -> p k c", p=P)

        def node_rows(table, j):
            return table[bass.ds(j * GROUP, GROUP), :].rearrange("(p k) c -> p k c", k=G)

        block = ctx.enter_context(nc.Block())

        full_tiles = E // P
        rest = E - full_tiles * P
        groups = []
        for g in range(4):
            t0 = g * TG
            n = max(0, min(TG, full_tiles - t0))
            groups.append((t0, n, rest if 0 <= full_tiles - t0 < TG else 0))
        n_loads = 0
        for t0, n, r in groups:
            n_loads += 2 * ((n > 0) + (r > 0))
            n_loads += (1 if t0 in (0, 2 * TG) else 0) + (n > (t0 in (0, 2 * TG))) + (r > 0)
        n_loads += 2 + 3 + 3 + G

        @block.sync
        def _(sp):
            sp.wait_ge(pads_set, 1)
            n = 0
            for g, (t0, full, r) in enumerate(groups):
                for a, table in enumerate((src, dst)):
                    if full:
                        sp.dma_start(raw[0:full, a, g, :], table[t0 * P:(t0 + full) * P].rearrange(
                            "(t e) -> t e", e=P)).then_inc(loaded, 16)
                        n += 1
                    if r:
                        e0 = (t0 + full) * P
                        sp.dma_start(raw[full:full + 1, a, g, 0:r], table[e0:e0 + r].rearrange(
                            "(t e) -> t e", t=1)).then_inc(loaded, 16)
                        n += 1
                first = 0
                if t0 in (0, 2 * TG):
                    e0 = t0 * P
                    sp.dma_start(raw[0:1, 2, g, 1:P], dst[e0:e0 + P - 1].rearrange("(t e) -> t e", t=1)).then_inc(loaded, 16)
                    n += 1
                    first = 1
                if full > first:
                    e0 = (t0 + first) * P - 1
                    sp.dma_start(raw[first:full, 2, g, :], dst[e0:e0 + (full - first) * P].rearrange(
                        "(t e) -> t e", e=P)).then_inc(loaded, 16)
                    n += 1
                if r:
                    e0 = (t0 + full) * P - 1
                    sp.dma_start(raw[full:full + 1, 2, g, 0:r], dst[e0:e0 + r].rearrange(
                        "(t e) -> t e", t=1)).then_inc(loaded, 16)
                    n += 1
            for c in range(2):
                sp.dma_start(mid_i[:, c:c + 1], dst[MID - 1 + c:MID + c].rearrange("(a b) -> a b", a=1).broadcast_to((P, 1))).then_inc(loaded, 16)
                n += 1
            for c, v in enumerate((b1, g1, be1)):
                sp.dma_start(vecs[:, c:c + 1], v.rearrange("(p a) -> p a", a=1)).then_inc(loaded, 16)
                n += 1
            sp.dma_start(w1_in[:, 0, :], W1).then_inc(loaded, 16)
            sp.dma_start(w1_in[:, 1, :], W1).then_inc(loaded, 16)
            sp.dma_start(w2_in[:, :], W2).then_inc(loaded, 16)
            n += 3
            for k in range(G):
                sp.dma_start(b2_row[:, k, :], b2.rearrange("(a c) -> a c", a=1)).then_inc(loaded, 16)
                n += 1
            assert n == n_loads
            sp.wait_ge(zero_set, 1)
            sp.dma_start(seg_rows[ZERO_ROW:ZERO_ROW + 2, :], zero_row[:, :]).then_inc(merged_stored, 16)

            sp.wait_ge(masks_made, 2)
            for q in range(2):
                for h in range(2):
                    sp.dma_start(mask_dram[2 * q + h, :].rearrange("(g t e) -> t g e", g=2, e=P),
                                 same_rows[0:TG, q, 2 * h:2 * h + 2, :]).then_inc(masks_out, 16)
            sp.wait_ge(masks_out, 64)
            sp.dma_start(masks[:, :], mask_dram).then_inc(masks_here, 16)

            sp.wait_ge(idx_made, 1)

            def edges(slot):
                s = slot.step(0)
                if s:
                    wait(sp, summed, s.j - 1)
                    sp.dma_start(src_slot[:, s.slot, :], src_idx[:, bass.ds(s.j * G, G), :].rearrange(
                        "p k h -> p (k h)")).then_inc(src_here[s.slot], 16)
                    wait(sp, turned, s.j - 1)
                    if s.known and s.j == NI - 1:
                        e0 = HALF + s.j * GROUP
                        full = (E - e0) // P
                        more = E - e0 - full * P
                        sp.dma_start(e_sum[:, s.slot, :, 0, :], edge_rows(edge_attr, 0, s.j)).then_inc(attr_here[s.slot], 16)
                        sp.dma_start(e_sum[:, s.slot, 0:full, 1, :], edge_attr[e0:e0 + full * P, :].rearrange(
                            "(k p) c -> p k c", p=P)).then_inc(attr_here[s.slot], 16)
                        sp.dma_start(e_sum[0:more, s.slot, full, 1, :], edge_attr[e0 + full * P:E, :]).then_inc(
                            attr_here[s.slot], 16)
                    else:
                        for half in range(2):
                            sp.dma_start(e_sum[:, s.slot, :, half, :], edge_rows(edge_attr, half, s.j)).then_inc(
                                attr_here[s.slot], 16)
                s = slot.step(-5)
                if s:
                    wait(sp, rows_made, s.j + 1)
                    for half in range(2):
                        sp.dma_start(edge_rows(seg_rows, half, s.j), row_out[:, s.slot, :, half, :]).then_inc(
                            rows_stored[s.slot], 16)

            pipeline(sp, edges, NI, 2, 0, 5)

            sp.wait_ge(rows_stored[0], 32 * ((NI + 1) // 2))
            sp.wait_ge(rows_stored[1], 32 * (NI // 2))
            sp.wait_ge(m_dve, 9)
            sp.wait_ge(merged_stored, 16)
            row = sp.value_load(mid_int[0:1, 3:4], min_val=0, max_val=SPARE_ROW)
            sp.dma_start(seg_rows[bass.ds(row, 1), :].rearrange("a c -> c a"), mrg[0:C, 15:16],
                         allow_slow_non_contiguous=True).then_inc(merged_stored, 16)

            sp.wait_ge(p_dve, 10)

            def nodes(slot):
                s = slot.step(0)
                if s:
                    wait(sp, o_summed, s.j - 3)
                    sp.dma_start(last_slot[:, s.slot, :], last_edge[:, bass.ds(s.j, 1), :].rearrange(
                        "p b k -> p (b k)")).then_inc(last_here[s.slot], 16)
                    wait(sp, z_made, s.j - 3)
                    if s.known and s.j == NB - 1:
                        sp.dma_start(x_in[0:tail_nodes, s.slot, :, :], x[s.j * GROUP:N, :].rearrange(
                            "(p k) c -> p k c", k=G)).then_inc(x_here[s.slot], 16)
                    else:
                        sp.dma_start(x_in[:, s.slot, :, :], node_rows(x, s.j)).then_inc(x_here[s.slot], 16)
                s = slot.step(-6)
                if s:
                    wait(sp, normed, s.j + 1)
                    if s.known and s.j == NB - 1:
                        sp.dma_start(out[s.j * GROUP:N, :].rearrange("(p k) c -> p k c", k=G),
                                     res[0:tail_nodes, s.slot, :, :]).then_inc(out_stored[s.slot], 16)
                    else:
                        sp.dma_start(node_rows(out, s.j), res[:, s.slot, :, :]).then_inc(out_stored[s.slot], 16)

            pipeline(sp, nodes, NB, 4, 0, 6)
            for i in range(4):
                sp.wait_ge(out_stored[i], 16 * len(range(i, NB, 4)))

        @block.gpsimd
        def _(pool):
            nc.gpsimd.memset(raw[:, 0, :, :], 0).then_inc(ramps_made, 1)
            nc.gpsimd.memset(raw[:, 1, :, :], 65535).then_inc(ramps_made, 1)
            nc.gpsimd.memset(raw[:, 2, :, :], -1).then_inc(ramps_made, 1)
            pool.wait_ge(ramps_made, 3)
            nc.gpsimd.memset(zero_row[:, :], 0.0).then_inc(pads_set, 1)
            nc.gpsimd.iota(ramp[:, :], [[1, P]], base=0, channel_multiplier=-1,
                           allow_small_or_imprecise_dtypes=True).then_inc(ramps_made, 1)
            nc.gpsimd.iota(node_ramp[:, :], [[1, P]], base=0, channel_multiplier=0,
                           allow_small_or_imprecise_dtypes=True).then_inc(ramps_made, 1)
            nc.gpsimd.iota(col_ramp[:, :], [[1, NC]], base=-(NC // 2), channel_multiplier=0,
                           allow_small_or_imprecise_dtypes=True).then_inc(ramps_made, 1)
            pool.wait_ge(pads_set, 1)
            nc.gpsimd.memset(snap[:, :, :], 0.0).then_inc(zero_set, 1)

            def edges(slot):
                s = slot.step(0)
                if s:
                    pool.wait_ge(src_here[s.slot], 16 * s.turn + 16)
                    wait(pool, summed, s.j - 1)
                    pool.sem_inc(gathers_open, 1)
                    for k in range(G):
                        for half in range(2):
                            n = 2 * k + half
                            nc.gpsimd.indirect_dma_start(
                                out=x_src[:, s.slot, k, half, :], out_offset=None, in_=x,
                                in_offset=bass.IndirectOffsetOnAxis(ap=src_slot[:, s.slot, n:n + 1], axis=0),
                            ).then_inc(gathered[s.slot], 16)

            pipeline(pool, edges, NI, 2, 0, 0)

            pool.wait_ge(rows_stored[0], 32 * ((NI + 1) // 2))
            pool.wait_ge(rows_stored[1], 32 * (NI // 2))
            pool.wait_ge(merged_stored, 32)

            def nodes(slot):
                s = slot.step(0)
                if s:
                    pool.wait_ge(last_here[s.slot], 16 * s.turn + 16)
                    wait(pool, o_summed, s.j - 3)
                    pool.sem_inc(gathers_open, 1)
                    for k in range(G):
                        nc.gpsimd.indirect_dma_start(
                            out=agg[:, s.slot, k, :], out_offset=None, in_=seg_rows,
                            in_offset=bass.IndirectOffsetOnAxis(ap=last_slot[:, s.slot, k:k + 1], axis=0),
                        ).then_inc(agg_here[s.slot], 16)

            pipeline(pool, nodes, NB, 4, 0, 0)

        @block.vector
        def _(dve):
            v = nc.vector
            steps = [0]

            def then(ins, last=True):
                steps[0] += 1
                ins.then_inc(prep, 1)
                if last:
                    dve.wait_ge(prep, steps[0])

            dve.wait_ge(ramps_made, 6)
            then(v.memset(ones[:, :], 1.0), last=False)
            then(v.memset(mean_w[:, :], 1.0 / P), last=False)
            then(v.memset(eps_col[:, 0:1], EPS), last=False)
            then(v.memset(eps_col[:, 1:2], LN_EPS), last=False)
            then(v.memset(state[:, 0, 0, 0:1], 0.0), last=False)
            then(v.tensor_scalar(ident[:, :], ramp[:, :], 0.0, None, ALU.is_equal), last=False)
            then(v.tensor_scalar(before_w[:, :], ramp[:, :], 0.0, None, ALU.is_gt), last=False)
            then(v.tensor_copy(node_ids[:, :], node_ramp[:, :]), last=False)
            then(v.tensor_copy(col_ids[:, :], col_ramp[:, :]))
            for a in range(2):
                for h in range(2):
                    then(v.tensor_copy(pick[:, a, h * C:(h + 1) * C],
                                       ident[0:4, 2 * a + h:2 * a + h + 1].broadcast_to((4, C))), last=False)
            then(v.tensor_scalar(minus_ident[:, :], ident[:, :], -1.0, None, ALU.mult), last=False)
            then(v.tensor_scalar(center[:, :], ident[:, :], -1.0 / P, None, ALU.add), last=False)
            dve.wait_ge(prep, steps[0])
            dve.wait_ge(loaded, 16 * n_loads)
            v.tensor_copy(rawf[:, :, :, :], raw[:, :, :, :]).then_inc(consts_made, 1)
            dve.wait_ge(consts_made, 1)
            v.tensor_tensor(same_rows[:, 0], rawf[:, 1], rawf[:, 2], ALU.is_equal).then_inc(masks_made, 1)
            dve.wait_ge(masks_made, 1)
            v.tensor_scalar(same_rows[:, 1], same_rows[:, 0], -1.0, NEVER, ALU.add, ALU.mult).then_inc(masks_made, 1)
            dve.wait_ge(idx_turned, 1)

            def by_tile(t):
                return t[:, :, :].rearrange("p (g t) h -> p h g t", g=2)

            def idx(a):
                return idx_ps[:, a, :, :].rearrange("p (h g) t -> p h g t", h=2)

            for h in range(2):
                then(v.tensor_copy(by_tile(src_idx)[:, h], idx(0)[:, h]), last=False)
                then(v.tensor_copy(by_tile(dst_f)[:, h], idx(1)[:, h]), last=False)
                then(v.tensor_copy(by_tile(dst_i)[:, h], idx(1)[:, h]), last=h == 1)
            then(v.tensor_scalar(int_a[:, :, :], dst_i[:, :, :], 2, P - 1, ALU.arith_shift_right, ALU.bitwise_and))
            then(v.tensor_copy(dst_p[:, :, :], int_a[:, :, :]))
            then(v.tensor_scalar(int_a[:, :, :], dst_i[:, :, :], 9, None, ALU.arith_shift_right))
            then(v.tensor_scalar(dst_c[:, :, :], int_a[:, :, :], float(G), float(-(NC // 2)), ALU.mult, ALU.add))
            then(v.tensor_scalar(int_a[:, :, :], dst_i[:, :, :], G - 1, None, ALU.bitwise_and))
            then(v.tensor_tensor(dst_c[:, :, :], dst_c[:, :, :], int_a[:, :, :], ALU.add))
            then(v.tensor_copy(mid_f[:, :], mid_i[:, :]))
            then(v.tensor_scalar(in_run[:, :], dst_f[:, :, 1], mid_f[:, 1:2], None, ALU.is_equal))
            v.tensor_reduce(mid_cnt[:, 0:1], in_run[:, :], AX_X, ALU.add).then_inc(idx_made, 1)
            dve.wait_ge(idx_made, 1)
            then(v.tensor_tensor(mid_cnt[:, 1:2], mid_f[:, 0:1], mid_f[:, 1:2], ALU.is_equal))
            dve.wait_ge(mid_counted, 1)
            then(v.tensor_scalar(mid_cnt[:, 2:3], small_ps[:, 0:1], -1.0, None, ALU.add))
            then(v.tensor_copy(mid_int[:, 0:1], mid_cnt[:, 2:3]))
            then(v.tensor_scalar(mid_int[:, 1:2], mid_int[:, 0:1], GROUP - 1, None, ALU.bitwise_and))
            then(v.tensor_scalar(mid_int[:, 2:3], mid_int[:, 0:1], GROUP.bit_length() - 1, None, ALU.arith_shift_right))
            then(v.tensor_scalar(mid_cnt[:, 3:4], mid_cnt[:, 2:3], float(MID - SPARE_ROW), None, ALU.add))
            then(v.tensor_tensor(mid_cnt[:, 3:4], mid_cnt[:, 3:4], mid_cnt[:, 1:2], ALU.mult))
            then(v.tensor_scalar(mid_int[:, 3:4], mid_cnt[:, 3:4], float(SPARE_ROW), None, ALU.add))
            dve.wait_ge(w_turned, 1)
            then(v.tensor_copy(w1_t[:, :], w_ps[:, 0:P]), last=False)
            then(v.tensor_copy(w2_t[:, :], w_ps[:, P:P + C]), last=False)
            v.tensor_copy(b1_c[:, :], w_ps[:, P + C:P + C + 1]).then_inc(w_made, 1)
            column = dve.value_load(mid_int[0:1, 1:2], min_val=0, max_val=GROUP - 1)

            def edges(slot):
                s = slot.step(1)
                if s:
                    dve.wait_ge(gathered[s.slot], 128 * s.turn + 128)
                    if s.known and s.j == NI - 1:
                        dve.wait_ge(attr_here[s.slot], 32 * s.turn + 48)
                    else:
                        dve.wait_ge(attr_here[s.slot], 32 * s.turn + 32)
                    v.tensor_tensor(e_sum[:, s.slot], e_sum[:, s.slot], x_src[:, s.slot], ALU.add).then_inc(summed, 1)
                s = slot.step(0)
                if s:
                    dve.wait_ge(turned, s.j + 1)
                    dve.wait_ge(same_copied, s.j + 1)
                    wait(dve, carried, s.j)
                    wait(dve, drop_made, s.j - 1)
                    wait(dve, snapped, s.j - 1)
                    v.tensor_tensor_scan(state[:, s.slot, 0, 1:], same_bc[:, s.slot, :], msg_ps[:, s.slot, :],
                                         state[:, s.slot, 0, 0:1], ALU.mult, ALU.max).then_inc(maxed, 1)
                r = slot.step(-1)
                if r:
                    dve.wait_ge(e_made, r.j + 1)
                    v.scalar_tensor_tensor(e_msg[:, r.slot, :], msg_ps[:, r.slot, :], 0.0, e_exp[:, r.slot, :],
                                           ALU.max, ALU.mult).then_inc(weighed, 1)
                    dve.wait_ge(c_made, r.j + 1)
                    wait(dve, log_made, r.j - 1)
                    first = r.known and r.j == 0
                    if not first:
                        dve.wait_ge(d_made, r.j)
                    v.tensor_tensor_scan(state[:, r.slot, 1, 1:], c_exp[:, r.slot, :], e_exp[:, r.slot, :],
                                         0.0 if first else state[:, 1 - r.slot, 1, GROUP:GROUP + 1],
                                         ALU.mult, ALU.add).then_inc(d_made, 1)
                if s and not (s.known and s.j == NI - 1):
                    dve.wait_ge(maxed, s.j + 1)
                    wait(dve, drop_made, s.j)
                    v.tensor_copy(state[:, 1 - s.slot, 0, 0:1], state[:, s.slot, 0, GROUP:GROUP + 1]).then_inc(carried, 1)
                if s:
                    dve.wait_ge(maxed, s.j + 1)
                    wait(dve, e_made, s.j - 1)
                    v.scalar_tensor_tensor(below[:, s.slot, :], msg_ps[:, s.slot, :], 0.0, state[:, s.slot, 0, 1:],
                                           ALU.max, ALU.subtract).then_inc(below_made, 1)
                    wait(dve, counted, s.j - 1)
                    for k in range(G):
                        for half in range(2):
                            n = 2 * k + half
                            v.tensor_scalar(hot_p[:, s.slot, n, :], node_ids[:, :], dst_p[:, bass.ds(s.j * G + k, 1), half],
                                            None, ALU.is_equal)
                            ins = v.tensor_scalar(hot_c[:, s.slot, n, :], col_ids[:, :],
                                                  dst_c[:, bass.ds(s.j * G + k, 1), half], None, ALU.is_equal)
                    ins.then_inc(hot_made, 1)
                if r:
                    dve.wait_ge(weighed, r.j + 1)
                    if not first:
                        dve.wait_ge(a_made, r.j)
                    v.tensor_tensor_scan(state[:, r.slot, 2, 1:], c_exp[:, r.slot, :], e_msg[:, r.slot, :],
                                         0.0 if first else state[:, 1 - r.slot, 2, GROUP:GROUP + 1],
                                         ALU.mult, ALU.add).then_inc(a_made, 1)
                q = slot.step(-2)
                if q:
                    dve.wait_ge(inv_made, q.j + 1)
                    wait(dve, turned_back, q.j - 1)
                    v.tensor_tensor(quot[:, q.slot, :], state[:, q.slot, 2, 1:], log_d[:, q.slot, :],
                                    ALU.mult).then_inc(divided, 1)
                if r:
                    dve.wait_ge(a_made, r.j + 1)
                    dve.wait_ge(d_made, r.j + 1)
                    v.tensor_copy(snap[C:P, bass.ds(r.j, 1), :].rearrange("p a q -> p (a q)"),
                                  state[C:P, r.slot, :, bass.ds(column + 1, 1)].rearrange("p q a -> p (q a)")).then_inc(snapped, 1)

            dve.wait_ge(zero_set, 1)
            pipeline(dve, edges, NI, 2, 1, 2)

            L = (NI - 1) % 2
            turn_of = dve.value_load(mid_int[0:1, 2:3], min_val=0, max_val=NI - 1)
            dve.wait_ge(snapped, NI)
            v.tensor_copy(mrg[:, 0:3], snap[:, bass.ds(turn_of, 1), :].rearrange("p a q -> p (a q)")).then_inc(m_dve, 1)
            dve.wait_ge(m_pe, 1)
            v.tensor_copy(mrg[0:C, 3:6], small_ps[0:C, 8:11]).then_inc(m_dve, 1)
            dve.wait_ge(m_dve, 2)
            v.tensor_tensor(mrg[0:C, 6:7], mrg[0:C, 3:4], state[0:C, L, 0, GROUP:GROUP + 1], ALU.max).then_inc(m_dve, 1)
            dve.wait_ge(m_dve, 3)
            v.tensor_tensor(mrg[0:C, 7:8], state[0:C, L, 0, GROUP:GROUP + 1], mrg[0:C, 6:7], ALU.subtract).then_inc(m_dve, 1)
            v.tensor_tensor(mrg[0:C, 8:9], mrg[0:C, 3:4], mrg[0:C, 6:7], ALU.subtract).then_inc(m_dve, 1)
            dve.wait_ge(m_act, 1)
            v.tensor_scalar(mrg[0:C, 11:13], state[0:C, L, 1:3, GROUP], mrg[0:C, 9:10], None, ALU.mult).then_inc(m_dve, 1)
            dve.wait_ge(m_dve, 6)
            v.scalar_tensor_tensor(mrg[0:C, 13:15], mrg[0:C, 4:6], mrg[0:C, 10:11], mrg[0:C, 11:13],
                                   ALU.mult, ALU.add).then_inc(m_dve, 1)
            dve.wait_ge(m_dve, 7)
            v.reciprocal(mrg[0:C, 12:13], mrg[0:C, 13:14]).then_inc(m_dve, 1)
            dve.wait_ge(m_dve, 8)
            v.tensor_scalar(mrg[0:C, 15:16], mrg[0:C, 14:15], mrg[0:C, 12:13], EPS, ALU.mult, ALU.add).then_inc(m_dve, 1)

            dve.wait_ge(counted, NI)
            v.tensor_copy(count[:, :, :], count_ps.rearrange("p (b k) -> p b k", k=G)).then_inc(p_dve, 1)
            dve.wait_ge(p_dve, 1)
            v.tensor_copy(upto[:, :, 0], count[:, :, 0]).then_inc(p_dve, 1)
            for k in range(1, G):
                dve.wait_ge(p_dve, k + 1)
                v.tensor_tensor(upto[:, :, k], upto[:, :, k - 1], count[:, :, k], ALU.add).then_inc(p_dve, 1)
            dve.wait_ge(p_pe, 1)
            v.tensor_copy(block_n[:, :], small_ps[:, 256:256 + NB]).then_inc(p_dve, 1)
            dve.wait_ge(p_dve, 6)
            v.tensor_tensor_scan(block_end[:, :], ones[:, 0:NB], block_n[:, :], 0.0, ALU.mult, ALU.add).then_inc(p_dve, 1)
            dve.wait_ge(p_dve, 7)
            v.tensor_tensor(block_0[:, :], block_end[:, :], block_n[:, :], ALU.subtract).then_inc(p_dve, 1)
            dve.wait_ge(p_dve, 8)
            v.tensor_tensor(block_0[:, :], block_0[:, :], small_ps[:, 128:128 + NB], ALU.add).then_inc(p_dve, 1)
            v.tensor_scalar(some[:, :, :], count[:, :, :], 0.0, None, ALU.is_gt)
            dve.wait_ge(p_dve, 9)
            v.tensor_tensor(upto[:, :, :], upto[:, :, :], block_0[:, :].rearrange("p (b a) -> p b a", a=1).broadcast_to(
                (P, NB, G)), ALU.add).then_inc(mid_made, 1)
            dve.wait_ge(mid_made, 1)
            v.scalar_tensor_tensor(upto[:, :, :], upto[:, :, :], float(-1 - ZERO_ROW), some[:, :, :],
                                   ALU.add, ALU.mult).then_inc(mid_made, 1)
            dve.wait_ge(mid_made, 2)
            v.tensor_scalar(last_edge[:, :, :], upto[:, :, :], float(ZERO_ROW), None, ALU.add).then_inc(p_dve, 1)

            def nodes(slot):
                s = slot.step(1)
                if s:
                    dve.wait_ge(agg_here[s.slot], 64 * s.turn + 64)
                    dve.wait_ge(x_here[s.slot], 16 * s.turn + 16)
                    wait(dve, o_turned, s.j - 3)
                    v.tensor_tensor(o_sum[:, s.slot], agg[:, s.slot], x_in[:, s.slot], ALU.add).then_inc(o_summed, 1)
                q = slot.step(-2)
                if q:
                    dve.wait_ge(z_squared, q.j + 1)
                    wait(dve, zlog_made, q.j - 1)
                    v.tensor_reduce(z_var[:, q.slot % 2, :], z_sq[:, q.slot % 2], AX_X, ALU.add).then_inc(zvar_made, 1)
                s = slot.step(0)
                if s:
                    dve.wait_ge(hinv_made, s.j + 1)
                    wait(dve, y_made, s.j - 1)
                    v.scalar_tensor_tensor(h_n[:, s.slot % 2].rearrange("p r q n -> p r (q n)"), h_ps[:, s.slot % 2],
                                           b1_c[:, 0:1], inv[:, s.slot % 2], ALU.add, ALU.mult).then_inc(h_scaled, 1)
                r = slot.step(-1)
                if r:
                    dve.wait_ge(y_made, r.j + 1)
                    v.tensor_tensor(z[:, r.slot], y_ps[:, r.slot % 2].rearrange("p (k c) -> p k c", k=G),
                                    x_in[:, r.slot], ALU.add).then_inc(z_made, 1)
                    dve.wait_ge(z_made, r.j + 1)
                    v.tensor_reduce(z_sum[:, r.slot % 2, :], z[:, r.slot], AX_X, ALU.add).then_inc(z_summed, 1)
                    dve.wait_ge(z_summed, r.j + 1)
                    v.scalar_tensor_tensor(z[:, r.slot], z_sum[:, r.slot % 2, :].rearrange("p (k a) -> p k a", a=1).broadcast_to(
                        (P, G, C)), -1.0 / C, z[:, r.slot], ALU.mult, ALU.add).then_inc(z_centered, 1)
                if q:
                    dve.wait_ge(zinv_made, q.j + 1)
                    wait(dve, out_stored[q.slot], 16 * q.turn)
                    v.tensor_tensor(res[:, q.slot], z[:, q.slot], z_inv[:, q.slot % 2, :].rearrange(
                        "p (k a) -> p k a", a=1).broadcast_to((P, G, C)), ALU.mult).then_inc(normed, 1)

            pipeline(dve, nodes, NB, 4, 1, 2)

        @block.tensor
        def _(pe):
            t = nc.tensor
            pe.wait_ge(consts_made, 1)
            for a in range(2):
                for g in range(4):
                    ins = t.transpose(idx_ps[:, a, g, :], rawf[0:TG, a, g, :], ident[0:TG, 0:TG])
            ins.then_inc(idx_turned, 1)
            t.matmul(w_ps[:, 0:P], w1_in[:, :, :].rearrange("p a c -> p (a c)"),
                     center[:, :], start=True, stop=True)
            t.matmul(w_ps[:, P + C:P + C + 1], center[:, :], vecs[:, 0:1], start=True, stop=True)
            t.transpose(w_ps[:, P:P + C], w2_in[:, :], ident[0:C, 0:C]).then_inc(w_turned, 1)
            pe.wait_ge(idx_made, 1)
            t.matmul(small_ps[:, 0:1], ones[:, :], mid_cnt[:, 0:1], start=True, stop=True).then_inc(mid_counted, 1)
            pe.wait_ge(w_made, 1)
            pe.wait_ge(masks_here, 16)
            def edges(slot):
                s = slot.step(1)
                if s:
                    pe.wait_ge(summed, s.j + 1)
                    wait(pe, weighed, s.j - 1)
                    for k in range(G):
                        ins = t.transpose(msg_ps[:, s.slot, k * P:(k + 1) * P],
                                          e_sum[:, s.slot, k].rearrange("p h c -> p (h c)"), ident[:, :])
                    ins.then_inc(turned, 1)
                    wait(pe, same_copied, s.j)
                    t.matmul(same_ps, pick[:, 0, :], masks[:, bass.ds(s.j * GROUP, GROUP)],
                             start=True, stop=True).then_inc(same_spread, 1)
                s = slot.step(0)
                if s:
                    pe.wait_ge(maxed, s.j + 1)
                    wait(pe, carried, s.j)
                    wait(pe, c_made, s.j - 1)
                    t.matmul(drop_ps[:, s.slot, :], ident[:, :], state[:, s.slot, 0, 0:GROUP], start=True, stop=False,
                             skip_group_check=True)
                    t.matmul(drop_ps[:, s.slot, :], minus_ident[:, :], state[:, s.slot, 0, 1:], start=False, stop=False,
                             skip_group_check=True)
                    t.matmul(drop_ps[:, s.slot, :], pick[:, 1, :], masks[:, bass.ds(s.j * GROUP, GROUP)],
                             start=False, stop=True, skip_group_check=True).then_inc(drop_made, 1)
                r = slot.step(-1)
                if r:
                    pe.wait_ge(hot_made, r.j + 1)
                    for n in range(2 * G):
                        ins = t.matmul(count_ps, hot_p[:, r.slot, n, :], hot_c[:, r.slot, n, :],
                                       start=(r.known and r.j == 0 and n == 0),
                                       stop=(r.known and r.j == NI - 1 and n == 2 * G - 1), skip_group_check=True)
                    ins.then_inc(counted, 1)
                q = slot.step(-2)
                if q:
                    pe.wait_ge(divided, q.j + 1)
                    wait(pe, rows_made, q.j)
                    for k in range(G):
                        ins = t.transpose(back_ps[:, k * P:(k + 1) * P], quot[:, q.slot, k * P:(k + 1) * P], ident[:, :])
                    ins.then_inc(turned_back, 1)

            pipeline(pe, edges, NI, 2, 1, 2)

            pe.wait_ge(m_dve, 1)
            t.matmul(small_ps[0:C, 8:11], ident[:, C:P], mrg[:, 0:3], start=True, stop=True).then_inc(m_pe, 1)
            pe.wait_ge(m_dve, 2)
            pe.wait_ge(p_dve, 5)
            t.matmul(small_ps[:, 128:128 + NB], before_w[:, :], upto[:, :, G - 1], start=True, stop=True)
            t.matmul(small_ps[:, 256:256 + NB], ones[:, :], upto[:, :, G - 1], start=True, stop=True).then_inc(p_pe, 1)
            pe.wait_ge(p_dve, 10)
            pe.wait_ge(rows_made, NI)
            pe.wait_ge(c_made, NI)
            pe.wait_ge(weighed, NI)

            def nodes(slot):
                s = slot.step(1)
                if s:
                    pe.wait_ge(o_summed, s.j + 1)
                    wait(pe, o_copied, s.j)
                    for q in range(2):
                        ins = t.transpose(ot_ps[:, q * P:(q + 1) * P],
                                          o_sum[:, s.slot, 2 * q:2 * q + 2, :].rearrange("p k c -> p (k c)"), ident[:, :])
                    ins.then_inc(o_turned, 1)
                c = slot.step(0)
                if c:
                    pe.wait_ge(sq_made, c.j + 1)
                    wait(pe, hlog_made, c.j)
                    t.matmul(var_ps, mean_w[:, :], sq[:, c.slot % 2].rearrange("p r n -> p (r n)"),
                             start=True, stop=True).then_inc(var_made, 1)
                r = slot.step(-1)
                if r:
                    wait(pe, z_made, r.j - 1)
                    t.matmul(y_ps[:, r.slot % 2], ones[0:1, :], b2_row[:, :, :].rearrange("p k c -> p (k c)"),
                             start=True, stop=False, skip_group_check=True)
                    pe.wait_ge(h_relu, r.j + 1)
                    for k in range(G):
                        ins = t.matmul(y_ps[:, r.slot % 2, k * C:(k + 1) * C], h_n[:, r.slot % 2, k % 2, k // 2, :],
                                       w2_t[:, :], start=False, stop=(k == G - 1), skip_group_check=True)
                    ins.then_inc(y_made, 1)
                if s:
                    pe.wait_ge(o_copied, s.j + 1)
                    wait(pe, h_scaled, s.j - 1)
                    for half in range(2):
                        rows = slice(half * C, half * C + C)
                        ins = t.matmul(h_ps[:, s.slot % 2, half, :], w1_t[rows, :],
                                       o_t[rows, s.slot % 2].rearrange("p q n -> p (q n)"), start=True, stop=True)
                    ins.then_inc(h_made, 1)

            pipeline(pe, nodes, NB, 4, 1, 2)

        @block.scalar
        def _(act):
            a = nc.scalar

            def edges(slot):
                s = slot.step(1)
                if s:
                    act.wait_ge(same_spread, s.j + 1)
                    wait(act, maxed, s.j - 1)
                    a.activation(same_bc[:, s.slot, :], same_ps, ACT.Copy).then_inc(same_copied, 1)
                s = slot.step(0)
                if s:
                    act.wait_ge(drop_made, s.j + 1)
                    wait(act, a_made, s.j - 1)
                    a.activation(c_exp[:, s.slot, :], drop_ps[:, s.slot, :], ACT.Exp).then_inc(c_made, 1)
                    act.wait_ge(below_made, s.j + 1)
                    a.activation(e_exp[:, s.slot, :], below[:, s.slot, :], ACT.Exp).then_inc(e_made, 1)
                r = slot.step(-1)
                if r:
                    act.wait_ge(d_made, r.j + 1)
                    wait(act, divided, r.j - 1)
                    a.activation(log_d[:, r.slot, :], state[:, r.slot, 1, 1:], ACT.Ln).then_inc(log_made, 1)
                    act.wait_ge(log_made, r.j + 1)
                    a.activation(log_d[:, r.slot, :], log_d[:, r.slot, :], ACT.Exp, scale=-1.0).then_inc(inv_made, 1)
                q = slot.step(-2)
                if q:
                    act.wait_ge(turned_back, q.j + 1)
                    wait(act, rows_stored[q.slot], 32 * q.turn)
                    a.activation(row_out[:, q.slot].rearrange("p k h c -> p (k h c)"), back_ps, ACT.Identity,
                                 bias=eps_col[:, 0:1]).then_inc(rows_made, 1)

            pipeline(act, edges, NI, 2, 1, 2)
            act.wait_ge(m_dve, 5)
            a.activation(mrg[0:C, 9:11], mrg[0:C, 7:9], ACT.Exp).then_inc(m_act, 1)

            def nodes(slot):
                q = slot.step(-2)
                if q:
                    act.wait_ge(z_centered, q.j + 1)
                    wait(act, zvar_made, q.j - 1)
                    a.activation(z_sq[:, q.slot % 2], z[:, q.slot], ACT.Square).then_inc(z_squared, 1)
                r = slot.step(-1)
                if r:
                    act.wait_ge(h_scaled, r.j + 1)
                    hv = h_n[:, r.slot % 2].rearrange("p r q n -> p (r q n)")
                    a.activation(hv, hv, ACT.Relu, bias=vecs[:, 2:3], scale=vecs[:, 1:2]).then_inc(h_relu, 1)
                s = slot.step(1)
                if s:
                    act.wait_ge(o_turned, s.j + 1)
                    wait(act, h_made, s.j - 1)
                    a.activation(o_t[:, s.slot % 2].rearrange("p q n -> p (q n)"), ot_ps, ACT.Copy).then_inc(o_copied, 1)
                c = slot.step(0)
                if c:
                    act.wait_ge(var_made, c.j + 1)
                    wait(act, h_scaled, c.j - 1)
                    iv = inv[:, c.slot % 2].rearrange("p r n -> p (r n)")
                    a.activation(iv, var_ps, ACT.Ln, bias=eps_col[:, 1:2]).then_inc(hlog_made, 1)
                    act.wait_ge(hlog_made, c.j + 1)
                    a.activation(iv, iv, ACT.Exp, scale=-0.5).then_inc(hinv_made, 1)
                if q:
                    act.wait_ge(zvar_made, q.j + 1)
                    wait(act, normed, q.j - 1)
                    a.activation(z_log[:, q.slot % 2, :], z_var[:, q.slot % 2, :], ACT.Ln, bias=eps_col[:, 1:2],
                                 scale=1.0 / C).then_inc(zlog_made, 1)
                    act.wait_ge(zlog_made, q.j + 1)
                    a.activation(z_inv[:, q.slot % 2, :], z_log[:, q.slot % 2, :], ACT.Exp, scale=-0.5).then_inc(zinv_made, 1)
                if s:
                    act.wait_ge(h_made, s.j + 1)
                    wait(act, var_made, s.j - 1)
                    a.activation(sq[:, s.slot % 2], h_ps[:, s.slot % 2], ACT.Square, bias=b1_c[:, 0:1]).then_inc(sq_made, 1)

            pipeline(act, nodes, NB, 4, 1, 2)


_INS = ['x', 'src', 'dst', 'edge_attr_64', 'L0_gnn_W1', 'L0_gnn_b1', 'L0_gnn_g1', 'L0_gnn_be1', 'L0_gnn_W2', 'L0_gnn_b2']
_OUTS = [((50000, 64), 'float32')]


def kernel(**inputs):
    import numpy as _np
    import concourse.bacc as _bacc
    from concourse import mybir as _mybir
    from concourse.bass_utils import run_bass_kernel_spmd as _run

    nc = _bacc.Bacc("TRN2", target_bir_lowering=False, num_devices=1)
    arrays, args = {}, []
    for name in _INS:
        a = _np.ascontiguousarray(inputs[name])
        arrays[f"in_{name}_dram"] = a
        args.append(nc.dram_tensor(f"in_{name}_dram", a.shape, _mybir.dt.from_np(a.dtype), kind="ExternalInput").ap())
    for i, (shape, dtype) in enumerate(_OUTS):
        dt = _mybir.dt.from_np(_np.dtype(dtype))
        args.append(nc.dram_tensor(f"out_{i}_dram", shape, dt, kind="ExternalOutput").ap())
    gnn_resnorm(nc, *args)
    r = _run(nc, [arrays], core_ids=[0])
    got = tuple(r.results[0][f"out_{i}_dram"] for i in range(len(_OUTS)))
    return got[0]
```

```python
from contextlib import ExitStack

import concourse.bass as bass
from concourse import mybir


P = 128
C = 64
G = 4
GROUP = P * G
EPS = 1e-07
LN_EPS = 1e-05
NEVER = 1e30

ALU = mybir.AluOpType
ACT = mybir.ActivationFunctionType
F32 = mybir.dt.float32
BF16 = mybir.dt.bfloat16
I32 = mybir.dt.int32
AX_X = mybir.AxisListType.X


class Step:

    def __init__(self, turn, place, ring):
        self.turn = turn + place // ring
        self.slot = place % ring
        self.j = self.turn * ring + self.slot
        self.known = isinstance(turn, int)


class Slot:

    def __init__(self, turn, place, ring, steps):
        self.turn, self.place, self.ring, self.steps = turn, place, ring, steps

    def step(self, off):
        s = Step(self.turn, self.place + off, self.ring)
        if s.known and not 0 <= s.j < self.steps:
            return None
        return s


def pipeline(engine, body, steps, ring, before, after):
    lo = -(-(after + 2) // ring)
    hi = (steps - before - 1) // ring
    for i in range(-before, lo * ring):
        body(Slot(i // ring, i % ring, ring, steps))
    with engine.Fori(lo, hi) as turn:
        for place in range(ring):
            body(Slot(turn, place, ring, steps))
    for i in range(hi * ring, steps + after):
        body(Slot(i // ring, i % ring, ring, steps))


def wait(engine, sem, n):
    if isinstance(n, int) and n <= 0:
        return
    engine.wait_ge(sem, n)


def gnn_resnorm(nc, x, src, dst, edge_attr, W1, b1, g1, be1, W2, b2, out):
    N = x.shape[0]
    E = src.shape[0]
    F = W1.shape[0]
    assert x.shape[1] == C and F == P
    HALF = -(-E // (2 * GROUP)) * GROUP
    NI = HALF // GROUP
    TILES = HALF // P
    TG = TILES // 2
    NB = -(-N // GROUP)
    NC = NB * G
    assert TG <= P and NC % 2 == 0 and NC // 2 <= 256 and NC <= 512 and N < 65535
    ZERO_ROW = 2 * HALF
    SPARE_ROW = 2 * HALF + 1
    R = 8
    MID = HALF
    tail_nodes = (N - (NB - 1) * GROUP) // G
    assert (N - (NB - 1) * GROUP) % G == 0

    mask_dram = nc.dram_tensor("mask_dram", (4, HALF), BF16, kind="Internal").ap()
    seg_rows = nc.dram_tensor("seg_rows", (2 * HALF + 2, C), F32, kind="Internal").ap()

    with ExitStack() as ctx:
        def sb(name, shape, dt=F32):
            return ctx.enter_context(nc.sbuf_tensor(name, shape, dt))

        def sem(name):
            return ctx.enter_context(nc.semaphore(name))

        psum = ctx.enter_context(nc.psum_tensor("psum", [P, 8, 512], F32))

        ramp = sb("ramp", [P, P])
        ident = sb("ident", [P, P])
        minus_ident = sb("minus_ident", [P, P])
        center = sb("center", [P, P])
        mean_w = sb("mean_w", [P, P])
        ones = sb("ones", [P, P])
        before_w = sb("before_w", [P, P])
        node_ramp = sb("node_ramp", [P, P])
        col_ramp = sb("col_ramp", [P, NC])
        node_ids = sb("node_ids", [P, P], BF16)
        col_ids = sb("col_ids", [P, NC], BF16)
        raw = sb("raw", [P, 3, 4, P], I32)
        rawf = sb("rawf", [P, 3, 4, P])
        src_idx = sb("src_idx", [P, TILES, 2], I32)
        dst_f = sb("dst_f", [P, TILES, 2])
        dst_i = sb("dst_i", [P, TILES, 2], I32)
        in_run = sb("in_run", [P, TILES])
        int_a = sb("int_a", [P, TILES, 2], I32)
        dst_p = sb("dst_p", [P, TILES, 2])
        dst_c = sb("dst_c", [P, TILES, 2])
        same_rows = sb("same_rows", [P, 2, 4, P], BF16)
        masks = sb("masks", [4, HALF], BF16)
        pick = sb("pick", [4, 2, P], BF16)
        mid_i = sb("mid_i", [P, 2], I32)
        mid_f = sb("mid_f", [P, 2])
        mid_cnt = sb("mid_cnt", [P, 4])
        mid_int = sb("mid_int", [P, 4], I32)
        w1_in = sb("w1_in", [P, 2, C])
        w2_in = sb("w2_in", [C, P])
        vecs = sb("vecs", [P, 3])
        w1_t = sb("w1_t", [P, 2, P])
        w2_t = sb("w2_t", [P, C])
        b1_c = sb("b1_c", [P, 1])
        b2_row = sb("b2_row", [1, G, C])
        b2_rest = sb("b2_rest", [1, 2, G, C])
        b2_part = sb("b2_part", [1, 3, G, C], BF16)
        ones_b = sb("ones_b", [1, P], BF16)
        eps_col = sb("eps_col", [P, 2])
        zero_row = sb("zero_row", [2, C])

        src_slot = sb("src_slot", [P, 2, 2 * G], I32)
        x_src = sb("x_src", [P, 2, G, 2, C])
        e_sum = sb("e_sum", [P, 2, G, 2, C])
        same_bc = sb("same_bc", [P, 2, GROUP])
        state = sb("state", [P, 2, 3, GROUP + 1])
        below = sb("below", [P, 2, GROUP])
        e_exp = sb("e_exp", [P, 2, GROUP])
        c_exp = sb("c_exp", [P, 2, GROUP])
        e_msg = sb("e_msg", [P, 2, GROUP])
        log_d = sb("log_d", [P, 2, GROUP])
        quot = sb("quot", [P, 2, GROUP])
        row_out = sb("row_out", [P, 2, G, 2, C])
        hot_p = sb("hot_p", [P, 2, 2 * G, P], BF16)
        hot_c = sb("hot_c", [P, 2, 2 * G, NC], BF16)
        snap = sb("snap", [P, NI, 3])
        mrg = sb("mrg", [P, 16])

        count = sb("count", [P, NB, G])
        upto = sb("upto", [P, NB, G])
        block_n = sb("block_n", [P, NB])
        block_end = sb("block_end", [P, NB])
        block_0 = sb("block_0", [P, NB])
        some = sb("some", [P, NB, G])
        last_edge = sb("last_edge", [P, NB, G], I32)
        last_slot = sb("last_slot", [P, 4, G], I32)
        agg = sb("agg", [P, 4, G, C])
        x_in = sb("x_in", [P, R, G, C])
        o_sum = sb("o_sum", [P, 4, G, C])
        o_t = sb("o_t", [P, 2, 2, P])
        sq = sb("sq", [P, 2, 2, 2 * P])
        inv = sb("inv", [P, 2, 2, 2 * P])
        h_n = sb("h_n", [P, 2, 2, 2, P])
        z = sb("z", [P, 4, G, C])
        z_sq = sb("z_sq", [P, 2, G, C])
        z_sum = sb("z_sum", [P, 2, G])
        z_var = sb("z_var", [P, 2, G])
        z_log = sb("z_log", [P, 2, G])
        z_inv = sb("z_inv", [P, 2, G])
        res = sb("res", [P, 4, G, C])

        pads_set = sem("pads_set")
        ramps_made = sem("ramps_made")
        loaded = sem("loaded")
        zero_set = sem("zero_set")
        prep = sem("prep")
        consts_made = sem("consts_made")
        masks_made = sem("masks_made")
        masks_out = sem("masks_out")
        masks_here = sem("masks_here")
        idx_turned = sem("idx_turned")
        idx_made = sem("idx_made")
        w_turned = sem("w_turned")
        w_made = sem("w_made")
        mid_counted = sem("mid_counted")
        mid_made = sem("mid_made")
        src_here = [sem(f"src_here{i}") for i in range(2)]
        attr_here = [sem(f"attr_here{i}") for i in range(2)]
        gathered = [sem(f"gathered{i}") for i in range(2)]
        gathers_open = sem("gathers_open")
        summed = sem("summed")
        turned = sem("turned")
        same_spread = sem("same_spread")
        same_copied = sem("same_copied")
        maxed = sem("maxed")
        carried = sem("carried")
        drop_made = sem("drop_made")
        below_made = sem("below_made")
        c_made = sem("c_made")
        e_made = sem("e_made")
        weighed = sem("weighed")
        d_made = sem("d_made")
        a_made = sem("a_made")
        snapped = sem("snapped")
        log_made = sem("log_made")
        inv_made = sem("inv_made")
        divided = sem("divided")
        turned_back = sem("turned_back")
        rows_made = sem("rows_made")
        rows_stored = [sem(f"rows_stored{i}") for i in range(2)]
        hot_made = sem("hot_made")
        counted = sem("counted")
        m_dve = sem("m_dve")
        m_pe = sem("m_pe")
        m_act = sem("m_act")
        merged_stored = sem("merged_stored")
        p_dve = sem("p_dve")
        p_pe = sem("p_pe")
        last_here = [sem(f"last_here{i}") for i in range(R)]
        x_here = [sem(f"x_here{i}") for i in range(R)]
        agg_here = [sem(f"agg_here{i}") for i in range(R)]
        o_summed = sem("o_summed")
        o_turned = sem("o_turned")
        o_copied = sem("o_copied")
        h_made = sem("h_made")
        sq_made = sem("sq_made")
        var_made = sem("var_made")
        hlog_made = sem("hlog_made")
        hinv_made = sem("hinv_made")
        h_scaled = sem("h_scaled")
        h_relu = sem("h_relu")
        y_made = sem("y_made")
        z_made = sem("z_made")
        z_summed = sem("z_summed")
        z_centered = sem("z_centered")
        z_squared = sem("z_squared")
        zvar_made = sem("zvar_made")
        zlog_made = sem("zlog_made")
        zinv_made = sem("zinv_made")
        normed = sem("normed")
        out_stored = [sem(f"out_stored{i}") for i in range(R)]

        idx_ps = psum[:, 0:2, 0:4 * TG].rearrange("p a (g t) -> p a g t", g=4)
        w_ps = psum[:, 3, :]
        msg_ps = psum[:, 0:2, :]
        same_ps = psum[:, 2, :]
        drop_ps = psum[:, 3:5, :]
        back_ps = psum[:, 5, :]
        count_ps = psum[:, 6, 0:NC]
        small_ps = psum[:, 7, :]
        ot_ps = psum[:, 0, 0:2 * P]
        h_ps = psum[:, 1:5, :].rearrange("p s (r n) -> p s r n", r=2)
        var_ps = psum[:, 5, :]
        y_ps = psum[:, 6:8, 0:G * C]

        def edge_rows(table, half, j):
            return table[bass.ds(j * GROUP + half * HALF, GROUP), :].rearrange("(k p) c -> p k c", p=P)

        def node_rows(table, j):
            return table[bass.ds(j * GROUP, GROUP), :].rearrange("(p k) c -> p k c", k=G)

        block = ctx.enter_context(nc.Block())

        full_tiles = E // P
        rest = E - full_tiles * P
        groups = []
        for g in range(4):
            t0 = g * TG
            n = max(0, min(TG, full_tiles - t0))
            groups.append((t0, n, rest if 0 <= full_tiles - t0 < TG else 0))
        n_loads = 0
        for t0, n, r in groups:
            n_loads += 2 * ((n > 0) + (r > 0))
            n_loads += (1 if t0 in (0, 2 * TG) else 0) + (n > (t0 in (0, 2 * TG))) + (r > 0)
        n_loads += 2 + 3 + 3 + G

        @block.sync
        def _(sp):
            sp.wait_ge(pads_set, 1)
            n = 0
            for g, (t0, full, r) in enumerate(groups):
                for a, table in enumerate((src, dst)):
                    if full:
                        sp.dma_start(raw[0:full, a, g, :], table[t0 * P:(t0 + full) * P].rearrange(
                            "(t e) -> t e", e=P)).then_inc(loaded, 16)
                        n += 1
                    if r:
                        e0 = (t0 + full) * P
                        sp.dma_start(raw[full:full + 1, a, g, 0:r], table[e0:e0 + r].rearrange(
                            "(t e) -> t e", t=1)).then_inc(loaded, 16)
                        n += 1
                first = 0
                if t0 in (0, 2 * TG):
                    e0 = t0 * P
                    sp.dma_start(raw[0:1, 2, g, 1:P], dst[e0:e0 + P - 1].rearrange("(t e) -> t e", t=1)).then_inc(loaded, 16)
                    n += 1
                    first = 1
                if full > first:
                    e0 = (t0 + first) * P - 1
                    sp.dma_start(raw[first:full, 2, g, :], dst[e0:e0 + (full - first) * P].rearrange(
                        "(t e) -> t e", e=P)).then_inc(loaded, 16)
                    n += 1
                if r:
                    e0 = (t0 + full) * P - 1
                    sp.dma_start(raw[full:full + 1, 2, g, 0:r], dst[e0:e0 + r].rearrange(
                        "(t e) -> t e", t=1)).then_inc(loaded, 16)
                    n += 1
            for c in range(2):
                sp.dma_start(mid_i[:, c:c + 1], dst[MID - 1 + c:MID + c].rearrange("(a b) -> a b", a=1).broadcast_to((P, 1))).then_inc(loaded, 16)
                n += 1
            for c, v in enumerate((b1, g1, be1)):
                sp.dma_start(vecs[:, c:c + 1], v.rearrange("(p a) -> p a", a=1)).then_inc(loaded, 16)
                n += 1
            sp.dma_start(w1_in[:, 0, :], W1).then_inc(loaded, 16)
            sp.dma_start(w1_in[:, 1, :], W1).then_inc(loaded, 16)
            sp.dma_start(w2_in[:, :], W2).then_inc(loaded, 16)
            n += 3
            for k in range(G):
                sp.dma_start(b2_row[:, k, :], b2.rearrange("(a c) -> a c", a=1)).then_inc(loaded, 16)
                n += 1
            assert n == n_loads
            sp.wait_ge(zero_set, 1)
            sp.dma_start(seg_rows[ZERO_ROW:ZERO_ROW + 2, :], zero_row[:, :]).then_inc(merged_stored, 16)

            sp.wait_ge(masks_made, 2)
            for q in range(2):
                for h in range(2):
                    sp.dma_start(mask_dram[2 * q + h, :].rearrange("(g t e) -> t g e", g=2, e=P),
                                 same_rows[0:TG, q, 2 * h:2 * h + 2, :]).then_inc(masks_out, 16)
            sp.wait_ge(masks_out, 64)
            sp.dma_start(masks[:, :], mask_dram).then_inc(masks_here, 16)

            sp.wait_ge(idx_made, 1)

            def edges(slot):
                s = slot.step(0)
                if s:
                    wait(sp, summed, s.j - 1)
                    sp.dma_start(src_slot[:, s.slot, :], src_idx[:, bass.ds(s.j * G, G), :].rearrange(
                        "p k h -> p (k h)")).then_inc(src_here[s.slot], 16)
                    wait(sp, turned, s.j - 1)
                    if s.known and s.j == NI - 1:
                        e0 = HALF + s.j * GROUP
                        full = (E - e0) // P
                        more = E - e0 - full * P
                        sp.dma_start(e_sum[:, s.slot, :, 0, :], edge_rows(edge_attr, 0, s.j)).then_inc(attr_here[s.slot], 16)
                        sp.dma_start(e_sum[:, s.slot, 0:full, 1, :], edge_attr[e0:e0 + full * P, :].rearrange(
                            "(k p) c -> p k c", p=P)).then_inc(attr_here[s.slot], 16)
                        sp.dma_start(e_sum[0:more, s.slot, full, 1, :], edge_attr[e0 + full * P:E, :]).then_inc(
                            attr_here[s.slot], 16)
                    else:
                        for half in range(2):
                            sp.dma_start(e_sum[:, s.slot, :, half, :], edge_rows(edge_attr, half, s.j)).then_inc(
                                attr_here[s.slot], 16)
                s = slot.step(-5)
                if s:
                    wait(sp, rows_made, s.j + 1)
                    for half in range(2):
                        sp.dma_start(edge_rows(seg_rows, half, s.j), row_out[:, s.slot, :, half, :]).then_inc(
                            rows_stored[s.slot], 16)

            pipeline(sp, edges, NI, 2, 0, 5)

            sp.wait_ge(rows_stored[0], 32 * ((NI + 1) // 2))
            sp.wait_ge(rows_stored[1], 32 * (NI // 2))
            sp.wait_ge(m_dve, 9)
            sp.wait_ge(merged_stored, 16)
            row = sp.value_load(mid_int[0:1, 3:4], min_val=0, max_val=SPARE_ROW)
            sp.dma_start(seg_rows[bass.ds(row, 1), :].rearrange("a c -> c a"), mrg[0:C, 15:16],
                         allow_slow_non_contiguous=True).then_inc(merged_stored, 16)

            sp.wait_ge(p_dve, 10)

            def nodes(slot):
                s = slot.step(0)
                if s:
                    wait(sp, o_summed, s.j - 3)
                    sp.dma_start(last_slot[:, s.slot % 4, :], last_edge[:, bass.ds(s.j, 1), :].rearrange(
                        "p b k -> p (b k)")).then_inc(last_here[s.slot], 16)
                    wait(sp, z_made, s.j - R + 1)
                    if s.known and s.j == NB - 1:
                        sp.dma_start(x_in[0:tail_nodes, s.slot, :, :], x[s.j * GROUP:N, :].rearrange(
                            "(p k) c -> p k c", k=G)).then_inc(x_here[s.slot], 16)
                    else:
                        sp.dma_start(x_in[:, s.slot, :, :], node_rows(x, s.j)).then_inc(x_here[s.slot], 16)
                s = slot.step(-10)
                if s:
                    wait(sp, normed, s.j + 1)
                    if s.known and s.j == NB - 1:
                        sp.dma_start(out[s.j * GROUP:N, :].rearrange("(p k) c -> p k c", k=G),
                                     res[0:tail_nodes, s.slot % 4, :, :]).then_inc(out_stored[s.slot], 16)
                    else:
                        sp.dma_start(node_rows(out, s.j), res[:, s.slot % 4, :, :]).then_inc(out_stored[s.slot], 16)

            pipeline(sp, nodes, NB, R, 0, 10)
            for i in range(R):
                sp.wait_ge(out_stored[i], 16 * len(range(i, NB, R)))

        @block.gpsimd
        def _(pool):
            nc.gpsimd.memset(raw[:, 0, :, :], 0).then_inc(ramps_made, 1)
            nc.gpsimd.memset(raw[:, 1, :, :], 65535).then_inc(ramps_made, 1)
            nc.gpsimd.memset(raw[:, 2, :, :], -1).then_inc(ramps_made, 1)
            pool.wait_ge(ramps_made, 3)
            nc.gpsimd.memset(zero_row[:, :], 0.0).then_inc(pads_set, 1)
            nc.gpsimd.iota(ramp[:, :], [[1, P]], base=0, channel_multiplier=-1,
                           allow_small_or_imprecise_dtypes=True).then_inc(ramps_made, 1)
            nc.gpsimd.iota(node_ramp[:, :], [[1, P]], base=0, channel_multiplier=0,
                           allow_small_or_imprecise_dtypes=True).then_inc(ramps_made, 1)
            nc.gpsimd.iota(col_ramp[:, :], [[1, NC]], base=-(NC // 2), channel_multiplier=0,
                           allow_small_or_imprecise_dtypes=True).then_inc(ramps_made, 1)
            pool.wait_ge(pads_set, 1)
            nc.gpsimd.memset(snap[:, :, :], 0.0).then_inc(zero_set, 1)

            def edges(slot):
                s = slot.step(0)
                if s:
                    pool.wait_ge(src_here[s.slot], 16 * s.turn + 16)
                    wait(pool, summed, s.j - 1)
                    pool.sem_inc(gathers_open, 1)
                    for k in range(G):
                        for half in range(2):
                            n = 2 * k + half
                            nc.gpsimd.indirect_dma_start(
                                out=x_src[:, s.slot, k, half, :], out_offset=None, in_=x,
                                in_offset=bass.IndirectOffsetOnAxis(ap=src_slot[:, s.slot, n:n + 1], axis=0),
                            ).then_inc(gathered[s.slot], 16)

            pipeline(pool, edges, NI, 2, 0, 0)

            pool.wait_ge(rows_stored[0], 32 * ((NI + 1) // 2))
            pool.wait_ge(rows_stored[1], 32 * (NI // 2))
            pool.wait_ge(merged_stored, 32)

            def nodes(slot):
                s = slot.step(0)
                if s:
                    pool.wait_ge(last_here[s.slot], 16 * s.turn + 16)
                    wait(pool, o_summed, s.j - 3)
                    pool.sem_inc(gathers_open, 1)
                    for k in range(G):
                        nc.gpsimd.indirect_dma_start(
                            out=agg[:, s.slot % 4, k, :], out_offset=None, in_=seg_rows,
                            in_offset=bass.IndirectOffsetOnAxis(ap=last_slot[:, s.slot % 4, k:k + 1], axis=0),
                        ).then_inc(agg_here[s.slot], 16)

            pipeline(pool, nodes, NB, R, 0, 0)

        @block.vector
        def _(dve):
            v = nc.vector
            steps = [0]

            def then(ins, last=True):
                steps[0] += 1
                ins.then_inc(prep, 1)
                if last:
                    dve.wait_ge(prep, steps[0])

            dve.wait_ge(ramps_made, 6)
            then(v.memset(ones[:, :], 1.0), last=False)
            then(v.memset(mean_w[:, :], 1.0 / P), last=False)
            then(v.memset(eps_col[:, 0:1], EPS), last=False)
            then(v.memset(eps_col[:, 1:2], LN_EPS), last=False)
            then(v.memset(state[:, 0, 0, 0:1], 0.0), last=False)
            then(v.tensor_scalar(ident[:, :], ramp[:, :], 0.0, None, ALU.is_equal), last=False)
            then(v.tensor_scalar(before_w[:, :], ramp[:, :], 0.0, None, ALU.is_gt), last=False)
            then(v.tensor_copy(node_ids[:, :], node_ramp[:, :]), last=False)
            then(v.tensor_copy(col_ids[:, :], col_ramp[:, :]))
            for a in range(2):
                for h in range(2):
                    then(v.tensor_copy(pick[:, a, h * C:(h + 1) * C],
                                       ident[0:4, 2 * a + h:2 * a + h + 1].broadcast_to((4, C))), last=False)
            then(v.tensor_scalar(minus_ident[:, :], ident[:, :], -1.0, None, ALU.mult), last=False)
            then(v.tensor_scalar(center[:, :], ident[:, :], -1.0 / P, None, ALU.add), last=False)
            dve.wait_ge(prep, steps[0])
            dve.wait_ge(loaded, 16 * n_loads)
            v.tensor_copy(rawf[:, :, :, :], raw[:, :, :, :]).then_inc(consts_made, 1)
            dve.wait_ge(consts_made, 1)
            v.tensor_tensor(same_rows[:, 0], rawf[:, 1], rawf[:, 2], ALU.is_equal).then_inc(masks_made, 1)
            dve.wait_ge(masks_made, 1)
            v.tensor_scalar(same_rows[:, 1], same_rows[:, 0], -1.0, NEVER, ALU.add, ALU.mult).then_inc(masks_made, 1)
            dve.wait_ge(idx_turned, 1)

            def by_tile(t):
                return t[:, :, :].rearrange("p (g t) h -> p h g t", g=2)

            def idx(a):
                return idx_ps[:, a, :, :].rearrange("p (h g) t -> p h g t", h=2)

            for h in range(2):
                then(v.tensor_copy(by_tile(src_idx)[:, h], idx(0)[:, h]), last=False)
                then(v.tensor_copy(by_tile(dst_f)[:, h], idx(1)[:, h]), last=False)
                then(v.tensor_copy(by_tile(dst_i)[:, h], idx(1)[:, h]), last=h == 1)
            then(v.tensor_scalar(int_a[:, :, :], dst_i[:, :, :], 2, P - 1, ALU.arith_shift_right, ALU.bitwise_and))
            then(v.tensor_copy(dst_p[:, :, :], int_a[:, :, :]))
            then(v.tensor_scalar(int_a[:, :, :], dst_i[:, :, :], 9, None, ALU.arith_shift_right))
            then(v.tensor_scalar(dst_c[:, :, :], int_a[:, :, :], float(G), float(-(NC // 2)), ALU.mult, ALU.add))
            then(v.tensor_scalar(int_a[:, :, :], dst_i[:, :, :], G - 1, None, ALU.bitwise_and))
            then(v.tensor_tensor(dst_c[:, :, :], dst_c[:, :, :], int_a[:, :, :], ALU.add))
            then(v.tensor_copy(mid_f[:, :], mid_i[:, :]))
            then(v.tensor_scalar(in_run[:, :], dst_f[:, :, 1], mid_f[:, 1:2], None, ALU.is_equal))
            v.tensor_reduce(mid_cnt[:, 0:1], in_run[:, :], AX_X, ALU.add).then_inc(idx_made, 1)
            dve.wait_ge(idx_made, 1)
            then(v.tensor_tensor(mid_cnt[:, 1:2], mid_f[:, 0:1], mid_f[:, 1:2], ALU.is_equal))
            dve.wait_ge(mid_counted, 1)
            then(v.tensor_scalar(mid_cnt[:, 2:3], small_ps[:, 0:1], -1.0, None, ALU.add))
            then(v.tensor_copy(mid_int[:, 0:1], mid_cnt[:, 2:3]))
            then(v.tensor_scalar(mid_int[:, 1:2], mid_int[:, 0:1], GROUP - 1, None, ALU.bitwise_and))
            then(v.tensor_scalar(mid_int[:, 2:3], mid_int[:, 0:1], GROUP.bit_length() - 1, None, ALU.arith_shift_right))
            then(v.tensor_scalar(mid_cnt[:, 3:4], mid_cnt[:, 2:3], float(MID - SPARE_ROW), None, ALU.add))
            then(v.tensor_tensor(mid_cnt[:, 3:4], mid_cnt[:, 3:4], mid_cnt[:, 1:2], ALU.mult))
            then(v.tensor_scalar(mid_int[:, 3:4], mid_cnt[:, 3:4], float(SPARE_ROW), None, ALU.add))
            dve.wait_ge(w_turned, 1)
            then(v.memset(w1_t[:, :, :], 0.0))
            for half in range(2):
                rows = slice(half * C, half * C + C)
                then(v.tensor_copy(w1_t[rows, half, :], w_ps[rows, 0:P]), last=False)
            then(v.tensor_copy(w2_t[:, :], w_ps[:, P:P + C]), last=False)
            then(v.memset(ones_b[:, :], 1.0), last=False)
            then(v.tensor_copy(b2_part[:, 0], b2_row[:, :, :]))
            then(v.tensor_tensor(b2_rest[:, 0], b2_row[:, :, :], b2_part[:, 0], ALU.subtract))
            then(v.tensor_copy(b2_part[:, 1], b2_rest[:, 0]))
            then(v.tensor_tensor(b2_rest[:, 1], b2_rest[:, 0], b2_part[:, 1], ALU.subtract))
            then(v.tensor_copy(b2_part[:, 2], b2_rest[:, 1]))
            v.tensor_copy(b1_c[:, :], w_ps[:, P + C:P + C + 1]).then_inc(w_made, 1)
            column = dve.value_load(mid_int[0:1, 1:2], min_val=0, max_val=GROUP - 1)

            def edges(slot):
                s = slot.step(1)
                if s:
                    dve.wait_ge(gathered[s.slot], 128 * s.turn + 128)
                    if s.known and s.j == NI - 1:
                        dve.wait_ge(attr_here[s.slot], 32 * s.turn + 48)
                    else:
                        dve.wait_ge(attr_here[s.slot], 32 * s.turn + 32)
                    v.tensor_tensor(e_sum[:, s.slot], e_sum[:, s.slot], x_src[:, s.slot], ALU.add).then_inc(summed, 1)
                s = slot.step(0)
                if s:
                    dve.wait_ge(turned, s.j + 1)
                    dve.wait_ge(same_copied, s.j + 1)
                    wait(dve, carried, s.j)
                    wait(dve, drop_made, s.j - 1)
                    wait(dve, snapped, s.j - 1)
                    v.tensor_tensor_scan(state[:, s.slot, 0, 1:], same_bc[:, s.slot, :], msg_ps[:, s.slot, :],
                                         state[:, s.slot, 0, 0:1], ALU.mult, ALU.max).then_inc(maxed, 1)
                r = slot.step(-1)
                if r:
                    dve.wait_ge(e_made, r.j + 1)
                    v.scalar_tensor_tensor(e_msg[:, r.slot, :], msg_ps[:, r.slot, :], 0.0, e_exp[:, r.slot, :],
                                           ALU.max, ALU.mult).then_inc(weighed, 1)
                    dve.wait_ge(c_made, r.j + 1)
                    wait(dve, log_made, r.j - 1)
                    first = r.known and r.j == 0
                    if not first:
                        dve.wait_ge(d_made, r.j)
                    v.tensor_tensor_scan(state[:, r.slot, 1, 1:], c_exp[:, r.slot, :], e_exp[:, r.slot, :],
                                         0.0 if first else state[:, 1 - r.slot, 1, GROUP:GROUP + 1],
                                         ALU.mult, ALU.add).then_inc(d_made, 1)
                if s and not (s.known and s.j == NI - 1):
                    dve.wait_ge(maxed, s.j + 1)
                    wait(dve, drop_made, s.j)
                    v.tensor_copy(state[:, 1 - s.slot, 0, 0:1], state[:, s.slot, 0, GROUP:GROUP + 1]).then_inc(carried, 1)
                if s:
                    dve.wait_ge(maxed, s.j + 1)
                    wait(dve, e_made, s.j - 1)
                    v.scalar_tensor_tensor(below[:, s.slot, :], msg_ps[:, s.slot, :], 0.0, state[:, s.slot, 0, 1:],
                                           ALU.max, ALU.subtract).then_inc(below_made, 1)
                    wait(dve, counted, s.j - 1)
                    for k in range(G):
                        for half in range(2):
                            n = 2 * k + half
                            v.tensor_scalar(hot_p[:, s.slot, n, :], node_ids[:, :], dst_p[:, bass.ds(s.j * G + k, 1), half],
                                            None, ALU.is_equal)
                            ins = v.tensor_scalar(hot_c[:, s.slot, n, :], col_ids[:, :],
                                                  dst_c[:, bass.ds(s.j * G + k, 1), half], None, ALU.is_equal)
                    ins.then_inc(hot_made, 1)
                if r:
                    dve.wait_ge(weighed, r.j + 1)
                    if not first:
                        dve.wait_ge(a_made, r.j)
                    v.tensor_tensor_scan(state[:, r.slot, 2, 1:], c_exp[:, r.slot, :], e_msg[:, r.slot, :],
                                         0.0 if first else state[:, 1 - r.slot, 2, GROUP:GROUP + 1],
                                         ALU.mult, ALU.add).then_inc(a_made, 1)
                q = slot.step(-2)
                if q:
                    dve.wait_ge(inv_made, q.j + 1)
                    wait(dve, turned_back, q.j - 1)
                    v.tensor_tensor(quot[:, q.slot, :], state[:, q.slot, 2, 1:], log_d[:, q.slot, :],
                                    ALU.mult).then_inc(divided, 1)
                if r:
                    dve.wait_ge(a_made, r.j + 1)
                    dve.wait_ge(d_made, r.j + 1)
                    v.tensor_copy(snap[C:P, bass.ds(r.j, 1), :].rearrange("p a q -> p (a q)"),
                                  state[C:P, r.slot, :, bass.ds(column + 1, 1)].rearrange("p q a -> p (q a)")).then_inc(snapped, 1)

            dve.wait_ge(zero_set, 1)
            pipeline(dve, edges, NI, 2, 1, 2)

            L = (NI - 1) % 2
            turn_of = dve.value_load(mid_int[0:1, 2:3], min_val=0, max_val=NI - 1)
            dve.wait_ge(snapped, NI)
            v.tensor_copy(mrg[:, 0:3], snap[:, bass.ds(turn_of, 1), :].rearrange("p a q -> p (a q)")).then_inc(m_dve, 1)
            dve.wait_ge(m_pe, 1)
            v.tensor_copy(mrg[0:C, 3:6], small_ps[0:C, 8:11]).then_inc(m_dve, 1)
            dve.wait_ge(m_dve, 2)
            v.tensor_tensor(mrg[0:C, 6:7], mrg[0:C, 3:4], state[0:C, L, 0, GROUP:GROUP + 1], ALU.max).then_inc(m_dve, 1)
            dve.wait_ge(m_dve, 3)
            v.tensor_tensor(mrg[0:C, 7:8], state[0:C, L, 0, GROUP:GROUP + 1], mrg[0:C, 6:7], ALU.subtract).then_inc(m_dve, 1)
            v.tensor_tensor(mrg[0:C, 8:9], mrg[0:C, 3:4], mrg[0:C, 6:7], ALU.subtract).then_inc(m_dve, 1)
            dve.wait_ge(m_act, 1)
            v.tensor_scalar(mrg[0:C, 11:13], state[0:C, L, 1:3, GROUP], mrg[0:C, 9:10], None, ALU.mult).then_inc(m_dve, 1)
            dve.wait_ge(m_dve, 6)
            v.scalar_tensor_tensor(mrg[0:C, 13:15], mrg[0:C, 4:6], mrg[0:C, 10:11], mrg[0:C, 11:13],
                                   ALU.mult, ALU.add).then_inc(m_dve, 1)
            dve.wait_ge(m_dve, 7)
            v.reciprocal(mrg[0:C, 12:13], mrg[0:C, 13:14]).then_inc(m_dve, 1)
            dve.wait_ge(m_dve, 8)
            v.tensor_scalar(mrg[0:C, 15:16], mrg[0:C, 14:15], mrg[0:C, 12:13], EPS, ALU.mult, ALU.add).then_inc(m_dve, 1)

            dve.wait_ge(counted, NI)
            v.tensor_copy(count[:, :, :], count_ps.rearrange("p (b k) -> p b k", k=G)).then_inc(p_dve, 1)
            dve.wait_ge(p_dve, 1)
            v.tensor_copy(upto[:, :, 0], count[:, :, 0]).then_inc(p_dve, 1)
            for k in range(1, G):
                dve.wait_ge(p_dve, k + 1)
                v.tensor_tensor(upto[:, :, k], upto[:, :, k - 1], count[:, :, k], ALU.add).then_inc(p_dve, 1)
            dve.wait_ge(p_pe, 1)
            v.tensor_copy(block_n[:, :], small_ps[:, 256:256 + NB]).then_inc(p_dve, 1)
            dve.wait_ge(p_dve, 6)
            v.tensor_tensor_scan(block_end[:, :], ones[:, 0:NB], block_n[:, :], 0.0, ALU.mult, ALU.add).then_inc(p_dve, 1)
            dve.wait_ge(p_dve, 7)
            v.tensor_tensor(block_0[:, :], block_end[:, :], block_n[:, :], ALU.subtract).then_inc(p_dve, 1)
            dve.wait_ge(p_dve, 8)
            v.tensor_tensor(block_0[:, :], block_0[:, :], small_ps[:, 128:128 + NB], ALU.add).then_inc(p_dve, 1)
            v.tensor_scalar(some[:, :, :], count[:, :, :], 0.0, None, ALU.is_gt)
            dve.wait_ge(p_dve, 9)
            v.tensor_tensor(upto[:, :, :], upto[:, :, :], block_0[:, :].rearrange("p (b a) -> p b a", a=1).broadcast_to(
                (P, NB, G)), ALU.add).then_inc(mid_made, 1)
            dve.wait_ge(mid_made, 1)
            v.scalar_tensor_tensor(upto[:, :, :], upto[:, :, :], float(-1 - ZERO_ROW), some[:, :, :],
                                   ALU.add, ALU.mult).then_inc(mid_made, 1)
            dve.wait_ge(mid_made, 2)
            v.tensor_scalar(last_edge[:, :, :], upto[:, :, :], float(ZERO_ROW), None, ALU.add).then_inc(p_dve, 1)

            def nodes(slot):
                s = slot.step(0)
                if s:
                    dve.wait_ge(agg_here[s.slot], 64 * s.turn + 64)
                    dve.wait_ge(x_here[s.slot], 16 * s.turn + 16)
                    wait(dve, o_turned, s.j - 1)
                    v.tensor_tensor(o_sum[:, s.slot % 2], agg[:, s.slot % 4], x_in[:, s.slot], ALU.add).then_inc(o_summed, 1)
                s = slot.step(-3)
                if s:
                    dve.wait_ge(hinv_made, s.j + 1)
                    wait(dve, y_made, s.j - 1)
                    v.scalar_tensor_tensor(h_n[:, s.slot % 2].rearrange("p r q n -> p r (q n)"), h_ps[:, s.slot % 4],
                                           b1_c[:, 0:1], inv[:, s.slot % 2], ALU.add, ALU.mult).then_inc(h_scaled, 1)
                s = slot.step(-6)
                if s:
                    dve.wait_ge(zinv_made, s.j + 1)
                    if s.known:
                        t = s.j - 4
                        if t >= 0:
                            dve.wait_ge(out_stored[t % R], 16 * (t // R) + 16)
                    else:
                        dve.wait_ge(out_stored[(s.slot - 4) % R], 16 * (s.turn + (s.slot - 4) // R) + 16)
                    v.tensor_tensor(res[:, s.slot % 4], z[:, s.slot % 4], z_inv[:, s.slot % 2, :].rearrange(
                        "p (k a) -> p k a", a=1).broadcast_to((P, G, C)), ALU.mult).then_inc(normed, 1)
                s = slot.step(-4)
                if s:
                    dve.wait_ge(y_made, s.j + 1)
                    v.tensor_tensor(z[:, s.slot % 4], y_ps[:, s.slot % 2].rearrange("p (k c) -> p k c", k=G),
                                    x_in[:, s.slot], ALU.add).then_inc(z_made, 1)
                    dve.wait_ge(z_made, s.j + 1)
                    v.tensor_reduce(z_sum[:, s.slot % 2, :], z[:, s.slot % 4], AX_X, ALU.add).then_inc(z_summed, 1)
                    dve.wait_ge(z_summed, s.j + 1)
                    v.scalar_tensor_tensor(z[:, s.slot % 4], z_sum[:, s.slot % 2, :].rearrange(
                        "p (k a) -> p k a", a=1).broadcast_to((P, G, C)), -1.0 / C, z[:, s.slot % 4],
                        ALU.mult, ALU.add).then_inc(z_centered, 1)
                s = slot.step(-5)
                if s:
                    dve.wait_ge(z_squared, s.j + 1)
                    wait(dve, zlog_made, s.j - 1)
                    v.tensor_reduce(z_var[:, s.slot % 2, :], z_sq[:, s.slot % 2], AX_X, ALU.add).then_inc(zvar_made, 1)

            pipeline(dve, nodes, NB, R, 0, 6)

        @block.tensor
        def _(pe):
            t = nc.tensor
            pe.wait_ge(consts_made, 1)
            for a in range(2):
                for g in range(4):
                    ins = t.transpose(idx_ps[:, a, g, :], rawf[0:TG, a, g, :], ident[0:TG, 0:TG])
            ins.then_inc(idx_turned, 1)
            t.matmul(w_ps[:, 0:P], w1_in[:, :, :].rearrange("p a c -> p (a c)"),
                     center[:, :], start=True, stop=True)
            t.matmul(w_ps[:, P + C:P + C + 1], center[:, :], vecs[:, 0:1], start=True, stop=True)
            t.transpose(w_ps[:, P:P + C], w2_in[:, :], ident[0:C, 0:C]).then_inc(w_turned, 1)
            pe.wait_ge(idx_made, 1)
            t.matmul(small_ps[:, 0:1], ones[:, :], mid_cnt[:, 0:1], start=True, stop=True).then_inc(mid_counted, 1)
            pe.wait_ge(w_made, 1)
            pe.wait_ge(masks_here, 16)
            def edges(slot):
                s = slot.step(1)
                if s:
                    pe.wait_ge(summed, s.j + 1)
                    wait(pe, weighed, s.j - 1)
                    for k in range(G):
                        ins = t.transpose(msg_ps[:, s.slot, k * P:(k + 1) * P],
                                          e_sum[:, s.slot, k].rearrange("p h c -> p (h c)"), ident[:, :])
                    ins.then_inc(turned, 1)
                    wait(pe, same_copied, s.j)
                    t.matmul(same_ps, pick[:, 0, :], masks[:, bass.ds(s.j * GROUP, GROUP)],
                             start=True, stop=True).then_inc(same_spread, 1)
                s = slot.step(0)
                if s:
                    pe.wait_ge(maxed, s.j + 1)
                    wait(pe, carried, s.j)
                    wait(pe, c_made, s.j - 1)
                    t.matmul(drop_ps[:, s.slot, :], ident[:, :], state[:, s.slot, 0, 0:GROUP], start=True, stop=False,
                             skip_group_check=True)
                    t.matmul(drop_ps[:, s.slot, :], minus_ident[:, :], state[:, s.slot, 0, 1:], start=False, stop=False,
                             skip_group_check=True)
                    t.matmul(drop_ps[:, s.slot, :], pick[:, 1, :], masks[:, bass.ds(s.j * GROUP, GROUP)],
                             start=False, stop=True, skip_group_check=True).then_inc(drop_made, 1)
                r = slot.step(-1)
                if r:
                    pe.wait_ge(hot_made, r.j + 1)
                    for n in range(2 * G):
                        ins = t.matmul(count_ps, hot_p[:, r.slot, n, :], hot_c[:, r.slot, n, :],
                                       start=(r.known and r.j == 0 and n == 0),
                                       stop=(r.known and r.j == NI - 1 and n == 2 * G - 1), skip_group_check=True)
                    ins.then_inc(counted, 1)
                q = slot.step(-2)
                if q:
                    pe.wait_ge(divided, q.j + 1)
                    wait(pe, rows_made, q.j)
                    for k in range(G):
                        ins = t.transpose(back_ps[:, k * P:(k + 1) * P], quot[:, q.slot, k * P:(k + 1) * P], ident[:, :])
                    ins.then_inc(turned_back, 1)

            pipeline(pe, edges, NI, 2, 1, 2)

            pe.wait_ge(m_dve, 1)
            t.matmul(small_ps[0:C, 8:11], ident[:, C:P], mrg[:, 0:3], start=True, stop=True).then_inc(m_pe, 1)
            pe.wait_ge(m_dve, 2)
            pe.wait_ge(p_dve, 5)
            t.matmul(small_ps[:, 128:128 + NB], before_w[:, :], upto[:, :, G - 1], start=True, stop=True)
            t.matmul(small_ps[:, 256:256 + NB], ones[:, :], upto[:, :, G - 1], start=True, stop=True).then_inc(p_pe, 1)
            pe.wait_ge(p_dve, 10)
            pe.wait_ge(rows_made, NI)
            pe.wait_ge(c_made, NI)
            pe.wait_ge(weighed, NI)

            def nodes(slot):
                s = slot.step(-4)
                if s:
                    wait(pe, z_made, s.j - 1)
                    for part in range(3):
                        t.matmul(y_ps[:, s.slot % 2], ones_b[:, :], b2_part[:, part].rearrange("p k c -> p (k c)"),
                                 start=(part == 0), stop=False, skip_group_check=True)
                    pe.wait_ge(h_relu, s.j + 1)
                    for k in range(G):
                        ins = t.matmul(y_ps[:, s.slot % 2, k * C:(k + 1) * C], h_n[:, s.slot % 2, k % 2, k // 2, :],
                                       w2_t[:, :], start=False, stop=(k == G - 1), skip_group_check=True)
                    ins.then_inc(y_made, 1)
                s = slot.step(-2)
                if s:
                    pe.wait_ge(sq_made, s.j + 1)
                    wait(pe, hlog_made, s.j)
                    t.matmul(var_ps, mean_w[:, :], sq[:, s.slot % 2].rearrange("p r n -> p (r n)"),
                             start=True, stop=True).then_inc(var_made, 1)
                s = slot.step(-1)
                if s:
                    pe.wait_ge(o_copied, s.j + 1)
                    wait(pe, h_scaled, s.j - 3)
                    for half in range(2):
                        ins = t.matmul(h_ps[:, s.slot % 4, half, :], w1_t[:, half, :],
                                       o_t[:, s.slot % 2].rearrange("p q n -> p (q n)"), start=True, stop=True)
                    ins.then_inc(h_made, 1)
                s = slot.step(0)
                if s:
                    pe.wait_ge(o_summed, s.j + 1)
                    wait(pe, o_copied, s.j)
                    for q in range(2):
                        ins = t.transpose(ot_ps[:, q * P:(q + 1) * P],
                                          o_sum[:, s.slot % 2, 2 * q:2 * q + 2, :].rearrange("p k c -> p (k c)"), ident[:, :])
                    ins.then_inc(o_turned, 1)

            pipeline(pe, nodes, NB, R, 0, 6)

        @block.scalar
        def _(act):
            a = nc.scalar
            a.preload_act_table_set("natural_log_exp_and_others")

            def edges(slot):
                s = slot.step(1)
                if s:
                    act.wait_ge(same_spread, s.j + 1)
                    wait(act, maxed, s.j - 1)
                    a.activation(same_bc[:, s.slot, :], same_ps, ACT.Copy).then_inc(same_copied, 1)
                s = slot.step(0)
                if s:
                    act.wait_ge(drop_made, s.j + 1)
                    wait(act, a_made, s.j - 1)
                    a.activation(c_exp[:, s.slot, :], drop_ps[:, s.slot, :], ACT.Exp).then_inc(c_made, 1)
                    act.wait_ge(below_made, s.j + 1)
                    a.activation(e_exp[:, s.slot, :], below[:, s.slot, :], ACT.Exp).then_inc(e_made, 1)
                r = slot.step(-1)
                if r:
                    act.wait_ge(d_made, r.j + 1)
                    wait(act, divided, r.j - 1)
                    a.activation(log_d[:, r.slot, :], state[:, r.slot, 1, 1:], ACT.Ln).then_inc(log_made, 1)
                    act.wait_ge(log_made, r.j + 1)
                    a.activation(log_d[:, r.slot, :], log_d[:, r.slot, :], ACT.Exp, scale=-1.0).then_inc(inv_made, 1)
                q = slot.step(-2)
                if q:
                    act.wait_ge(turned_back, q.j + 1)
                    wait(act, rows_stored[q.slot], 32 * q.turn)
                    a.activation(row_out[:, q.slot].rearrange("p k h c -> p (k h c)"), back_ps, ACT.Identity,
                                 bias=eps_col[:, 0:1]).then_inc(rows_made, 1)

            pipeline(act, edges, NI, 2, 1, 2)
            act.wait_ge(m_dve, 5)
            a.activation(mrg[0:C, 9:11], mrg[0:C, 7:9], ACT.Exp).then_inc(m_act, 1)

            def nodes(slot):
                s = slot.step(-3)
                if s:
                    act.wait_ge(h_scaled, s.j + 1)
                    hv = h_n[:, s.slot % 2].rearrange("p r q n -> p (r q n)")
                    a.activation(hv, hv, ACT.Relu, bias=vecs[:, 2:3], scale=vecs[:, 1:2]).then_inc(h_relu, 1)
                s = slot.step(-5)
                if s:
                    act.wait_ge(z_centered, s.j + 1)
                    wait(act, zvar_made, s.j - 1)
                    a.activation(z_sq[:, s.slot % 2], z[:, s.slot % 4], ACT.Square).then_inc(z_squared, 1)
                s = slot.step(-2)
                if s:
                    act.wait_ge(var_made, s.j + 1)
                    wait(act, h_scaled, s.j - 1)
                    iv = inv[:, s.slot % 2].rearrange("p r n -> p (r n)")
                    a.activation(iv, var_ps, ACT.Ln, bias=eps_col[:, 1:2]).then_inc(hlog_made, 1)
                    act.wait_ge(hlog_made, s.j + 1)
                    a.activation(iv, iv, ACT.Exp, scale=-0.5).then_inc(hinv_made, 1)
                s = slot.step(-1)
                if s:
                    act.wait_ge(h_made, s.j + 1)
                    wait(act, var_made, s.j - 1)
                    a.activation(sq[:, s.slot % 2], h_ps[:, s.slot % 4], ACT.Square, bias=b1_c[:, 0:1]).then_inc(sq_made, 1)
                s = slot.step(0)
                if s:
                    act.wait_ge(o_turned, s.j + 1)
                    wait(act, h_made, s.j - 1)
                    a.activation(o_t[:, s.slot % 2].rearrange("p q n -> p (q n)"), ot_ps, ACT.Copy).then_inc(o_copied, 1)
                s = slot.step(-5)
                if s:
                    act.wait_ge(zvar_made, s.j + 1)
                    wait(act, normed, s.j - 1)
                    a.activation(z_log[:, s.slot % 2, :], z_var[:, s.slot % 2, :], ACT.Ln, bias=eps_col[:, 1:2],
                                 scale=1.0 / C).then_inc(zlog_made, 1)
                    act.wait_ge(zlog_made, s.j + 1)
                    a.activation(z_inv[:, s.slot % 2, :], z_log[:, s.slot % 2, :], ACT.Exp, scale=-0.5).then_inc(zinv_made, 1)

            pipeline(act, nodes, NB, R, 0, 6)


_INS = ['x', 'src', 'dst', 'edge_attr_64', 'L0_gnn_W1', 'L0_gnn_b1', 'L0_gnn_g1', 'L0_gnn_be1', 'L0_gnn_W2', 'L0_gnn_b2']
_OUTS = [((50000, 64), 'float32')]


def kernel(**inputs):
    import numpy as _np
    import concourse.bacc as _bacc
    from concourse import mybir as _mybir
    from concourse.bass_utils import run_bass_kernel_spmd as _run

    nc = _bacc.Bacc("TRN2", target_bir_lowering=False, num_devices=1)
    arrays, args = {}, []
    for name in _INS:
        a = _np.ascontiguousarray(inputs[name])
        arrays[f"in_{name}_dram"] = a
        args.append(nc.dram_tensor(f"in_{name}_dram", a.shape, _mybir.dt.from_np(a.dtype), kind="ExternalInput").ap())
    for i, (shape, dtype) in enumerate(_OUTS):
        dt = _mybir.dt.from_np(_np.dtype(dtype))
        args.append(nc.dram_tensor(f"out_{i}_dram", shape, dt, kind="ExternalOutput").ap())
    gnn_resnorm(nc, *args)
    r = _run(nc, [arrays], core_ids=[0])
    got = tuple(r.results[0][f"out_{i}_dram"] for i in range(len(_OUTS)))
    return got[0]
```

```python
from contextlib import ExitStack

import concourse.bass as bass
from concourse import mybir


P = 128
C = 64
G = 4
GROUP = P * G
EPS = 1e-07
LN_EPS = 1e-05
NEVER = 1e30

ALU = mybir.AluOpType
ACT = mybir.ActivationFunctionType
F32 = mybir.dt.float32
BF16 = mybir.dt.bfloat16
I32 = mybir.dt.int32
AX_X = mybir.AxisListType.X


class Step:

    def __init__(self, turn, place, ring):
        self.turn = turn + place // ring
        self.slot = place % ring
        self.j = self.turn * ring + self.slot
        self.known = isinstance(turn, int)


class Slot:

    def __init__(self, turn, place, ring, steps):
        self.turn, self.place, self.ring, self.steps = turn, place, ring, steps

    def step(self, off):
        s = Step(self.turn, self.place + off, self.ring)
        if s.known and not 0 <= s.j < self.steps:
            return None
        return s


def pipeline(engine, body, steps, ring, before, after, back=0):
    lo = -(-(max(after, back) + 2) // ring)
    hi = (steps - before - 1) // ring
    for i in range(-before, lo * ring):
        body(Slot(i // ring, i % ring, ring, steps))
    with engine.Fori(lo, hi) as turn:
        for place in range(ring):
            body(Slot(turn, place, ring, steps))
    for i in range(hi * ring, steps + after):
        body(Slot(i // ring, i % ring, ring, steps))


def wait(engine, sem, n):
    if isinstance(n, int) and n <= 0:
        return
    engine.wait_ge(sem, n)


def gnn_resnorm(nc, x, src, dst, edge_attr, W1, b1, g1, be1, W2, b2, out):
    N = x.shape[0]
    E = src.shape[0]
    F = W1.shape[0]
    assert x.shape[1] == C and F == P
    HALF = -(-E // (2 * GROUP)) * GROUP
    NI = HALF // GROUP
    TILES = HALF // P
    TG = TILES // 2
    NB = -(-N // GROUP)
    NC = NB * G
    assert TG <= P and NC % 2 == 0 and NC // 2 <= 256 and NC <= 512 and N < 65535
    ZERO_ROW = 2 * HALF
    MERGED_ROW = 2 * HALF + 1
    NO_ROW = 2
    RE = 4
    R = 8
    EARLY = 3
    MID = HALF
    tail_nodes = (N - (NB - 1) * GROUP) // G
    assert (N - (NB - 1) * GROUP) % G == 0

    mask_dram = nc.dram_tensor("mask_dram", (4, HALF), BF16, kind="Internal").ap()
    seg_rows = nc.dram_tensor("seg_rows", (2 * HALF + 2, C), F32, kind="Internal").ap()

    with ExitStack() as ctx:
        def sb(name, shape, dt=F32):
            return ctx.enter_context(nc.sbuf_tensor(name, shape, dt))

        def sem(name):
            return ctx.enter_context(nc.semaphore(name))

        psum = ctx.enter_context(nc.psum_tensor("psum", [P, 8, 512], F32))

        ramp = sb("ramp", [P, P])
        ident = sb("ident", [P, P])
        minus_ident = sb("minus_ident", [P, P])
        center = sb("center", [P, P])
        mean_w = sb("mean_w", [P, P])
        ones = sb("ones", [P, P])
        before_w = sb("before_w", [P, P])
        node_ramp = sb("node_ramp", [P, P])
        col_ramp = sb("col_ramp", [P, NC])
        node_ids = sb("node_ids", [P, P], BF16)
        col_ids = sb("col_ids", [P, NC], BF16)
        raw = sb("raw", [P, 3, 4, P], I32)
        rawf = sb("rawf", [P, 3, 4, P])
        src_idx = sb("src_idx", [P, TILES, 2], I32)
        dst_f = sb("dst_f", [P, TILES, 2])
        dst_i = sb("dst_i", [P, TILES, 2], I32)
        in_run = sb("in_run", [P, TILES])
        int_a = sb("int_a", [P, TILES, 2], I32)
        minus_p = sb("minus_p", [P, TILES, 2])
        dst_c = sb("dst_c", [P, TILES, 2])
        same_rows = sb("same_rows", [P, 2, 4, P], BF16)
        masks = sb("masks", [4, HALF], BF16)
        pick = sb("pick", [4, 2, P], BF16)
        mid_i = sb("mid_i", [P, 2], I32)
        mid_f = sb("mid_f", [P, 2])
        mid_cnt = sb("mid_cnt", [P, 5])
        mid_int = sb("mid_int", [P, 3], I32)
        w1_in = sb("w1_in", [P, 2, C])
        w2_in = sb("w2_in", [C, P])
        vecs = sb("vecs", [P, 3])
        w1_t = sb("w1_t", [P, 2, P])
        w2_t = sb("w2_t", [P, C])
        b1_c = sb("b1_c", [P, 1])
        b2_row = sb("b2_row", [1, G, C])
        b2_rest = sb("b2_rest", [1, 2, G, C])
        b2_part = sb("b2_part", [1, 3, G, C], BF16)
        ones_b = sb("ones_b", [1, P], BF16)
        eps_col = sb("eps_col", [P, 2])
        zero_row = sb("zero_row", [1, C])

        src_slot = sb("src_slot", [P, RE, G, 2], I32)
        x_src = sb("x_src", [P, RE, G, 2, C])
        e_sum = sb("e_sum", [P, RE, G, 2, C])
        same_bc = sb("same_bc", [P, 2, GROUP])
        state = sb("state", [P, 2, 3, GROUP + 1])
        below = sb("below", [P, 2, GROUP])
        e_exp = sb("e_exp", [P, 2, GROUP])
        c_exp = sb("c_exp", [P, 2, GROUP])
        e_msg = sb("e_msg", [P, 2, GROUP])
        log_d = sb("log_d", [P, 2, GROUP])
        quot = sb("quot", [P, 2, GROUP])
        row_out = sb("row_out", [P, 2, G, 2, C])
        off_p = sb("off_p", [P, 2 * G, P], BF16)
        hot_p = sb("hot_p", [P, 2, 2 * G, P], BF16)
        hot_c = sb("hot_c", [P, 2, 2 * G, NC], BF16)
        one_col = sb("one_col", [P, 1])
        snap = sb("snap", [P, NI, 3])
        mrg = sb("mrg", [P, 16])

        count = sb("count", [P, NB, G])
        upto = sb("upto", [P, NB, G])
        block_n = sb("block_n", [P, NB])
        block_end = sb("block_end", [P, NB])
        block_0 = sb("block_0", [P, NB])
        some = sb("some", [P, NB, G])
        cut_row = sb("cut_row", [P, NB, G])
        last_edge = sb("last_edge", [P, NB, G], I32)
        last_slot = sb("last_slot", [P, 4, G], I32)
        agg = sb("agg", [P, 4, G, C])
        x_in = x_src[:, :, :, :, :].rearrange("p t k h c -> p (t k h c)").rearrange("p (r k c) -> p r k c", r=R, k=G)
        o_sum = sb("o_sum", [P, 4, G, C])
        o_t = sb("o_t", [P, 2, 2, P])
        sq = sb("sq", [P, 2, 2, 2 * P])
        inv = sb("inv", [P, 2, 2, 2 * P])
        h_n = sb("h_n", [P, 2, 2, 2, P])
        z = sb("z", [P, 4, G, C])
        z_sq = sb("z_sq", [P, 2, G, C])
        z_sum = sb("z_sum", [P, 2, G])
        z_var = sb("z_var", [P, 2, G])
        z_log = sb("z_log", [P, 2, G])
        z_inv = sb("z_inv", [P, 2, G])
        res = sb("res", [P, 4, G, C])

        pads_set = sem("pads_set")
        ramps_made = sem("ramps_made")
        tiles_loaded = sem("tiles_loaded")
        weights_loaded = sem("weights_loaded")
        mask_cut = sem("mask_cut")
        zero_set = sem("zero_set")
        prep = sem("prep")
        consts_made = sem("consts_made")
        masks_made = sem("masks_made")
        masks_out = sem("masks_out")
        masks_here = sem("masks_here")
        idx_turned = sem("idx_turned")
        idx_made = sem("idx_made")
        w_turned = sem("w_turned")
        w_made = sem("w_made")
        mid_counted = sem("mid_counted")
        mid_made = sem("mid_made")
        src_here = [sem(f"src_here{i}") for i in range(RE)]
        attr_here = [sem(f"attr_here{i}") for i in range(RE)]
        gathered = [sem(f"gathered{i}") for i in range(RE)]
        gathers_open = sem("gathers_open")
        e_summed = sem("e_summed")
        turned = sem("turned")
        same_spread = sem("same_spread")
        same_copied = sem("same_copied")
        maxed = sem("maxed")
        carried = sem("carried")
        drop_made = sem("drop_made")
        below_made = sem("below_made")
        c_made = sem("c_made")
        e_made = sem("e_made")
        weighed = sem("weighed")
        d_made = sem("d_made")
        a_made = sem("a_made")
        snapped = sem("snapped")
        log_made = sem("log_made")
        inv_made = sem("inv_made")
        divided = sem("divided")
        turned_back = sem("turned_back")
        rows_made = sem("rows_made")
        rows_stored = [sem(f"rows_stored{i}") for i in range(RE)]
        off_made = sem("off_made")
        hot_p_made = sem("hot_p_made")
        hot_c_made = sem("hot_c_made")
        counted = sem("counted")
        m_dve = sem("m_dve")
        m_pe = sem("m_pe")
        m_act = sem("m_act")
        merged_stored = sem("merged_stored")
        p_dve = sem("p_dve")
        p_pe = sem("p_pe")
        last_here = [sem(f"last_here{i}") for i in range(R)]
        x_here = [sem(f"x_here{i}") for i in range(R)]
        agg_here = [sem(f"agg_here{i}") for i in range(R)]
        o_summed = sem("o_summed")
        o_turned = sem("o_turned")
        o_copied = sem("o_copied")
        h_made = sem("h_made")
        sq_made = sem("sq_made")
        var_made = sem("var_made")
        hlog_made = sem("hlog_made")
        hinv_made = sem("hinv_made")
        h_scaled = sem("h_scaled")
        h_relu = sem("h_relu")
        y_made = sem("y_made")
        z_made = sem("z_made")
        z_summed = sem("z_summed")
        z_centered = sem("z_centered")
        z_squared = sem("z_squared")
        zvar_made = sem("zvar_made")
        zlog_made = sem("zlog_made")
        zinv_made = sem("zinv_made")
        normed = sem("normed")
        out_stored = [sem(f"out_stored{i}") for i in range(R)]

        idx_ps = psum[:, 0:2, 0:4 * TG].rearrange("p a (g t) -> p a g t", g=4)
        w_ps = psum[:, 3, :]
        msg_ps = psum[:, 0:2, :]
        same_ps = psum[:, 2, :]
        drop_ps = psum[:, 3:5, :]
        back_ps = psum[:, 5, :]
        count_ps = psum[:, 6, 0:NC]
        small_ps = psum[:, 7, :]
        ot_ps = psum[:, 0, 0:2 * P]
        h_ps = psum[:, 1:5, :].rearrange("p s (r n) -> p s r n", r=2)
        var_ps = psum[:, 5, :]
        y_ps = psum[:, 6:8, 0:G * C]

        def edge_rows(table, half, j):
            return table[bass.ds(j * GROUP + half * HALF, GROUP), :].rearrange("(k p) c -> p k c", p=P)

        def node_rows(table, j):
            return table[bass.ds(j * GROUP, GROUP), :].rearrange("(p k) c -> p k c", k=G)

        block = ctx.enter_context(nc.Block())

        full_tiles, rest = divmod(E, P)
        whole = full_tiles // TG
        over = full_tiles - whole * TG
        assert whole == 3

        def all_rows_stored(engine):
            for i in range(RE):
                engine.wait_ge(rows_stored[i], 32 * len(range(i, NI, RE)))

        def early(engine, j):
            for half in range(2):
                e0 = half * HALF + j * GROUP
                engine.dma_start(src_slot[:, j, :, half], src[e0:e0 + GROUP].rearrange("(k p) -> p k", p=P),
                                 allow_slow_non_contiguous=True).then_inc(src_here[j], 16)

        @block.sync
        def _(sp):
            def tiles(a, table, shift):
                if shift:
                    sp.dma_start(raw[0:1, a, 0, 1:P], table[0:P - 1].rearrange("(t e) -> t e", t=1)).then_inc(tiles_loaded, 16)
                    sp.dma_start(raw[1:TG, a, 0, :], table[P - 1:TG * P - 1].rearrange("(t e) -> t e", e=P)).then_inc(tiles_loaded, 16)
                g0 = 1 if shift else 0
                sp.dma_start(raw[0:TG, a, g0:whole, :], table[g0 * TG * P - shift:whole * TG * P - shift].rearrange(
                    "(g t e) -> t g e", e=P, t=TG)).then_inc(tiles_loaded, 16)
                e0 = whole * TG * P - shift
                sp.dma_start(raw[0:over, a, whole, :], table[e0:e0 + over * P].rearrange(
                    "(t e) -> t e", e=P)).then_inc(tiles_loaded, 16)
                e0 += over * P
                sp.dma_start(raw[over:over + 1, a, whole, 0:rest], table[e0:e0 + rest].rearrange(
                    "(t e) -> t e", t=1)).then_inc(tiles_loaded, 16)

            early(sp, 0)
            sp.wait_ge(pads_set, 1)
            tiles(1, dst, 0)
            tiles(2, dst, 1)
            tiles(0, src, 0)
            sp.wait_ge(zero_set, 1)
            sp.dma_start(seg_rows[ZERO_ROW:ZERO_ROW + 1, :], zero_row[:, :]).then_inc(merged_stored, 16)

            sp.wait_ge(masks_made, 2)
            for q in range(2):
                for h in range(2):
                    sp.dma_start(mask_dram[2 * q + h, :].rearrange("(g t e) -> t g e", g=2, e=P),
                                 same_rows[0:TG, q, 2 * h:2 * h + 2, :]).then_inc(masks_out, 16)
            sp.wait_ge(masks_out, 64)
            sp.dma_start(masks[:, :], mask_dram).then_inc(masks_here, 16)

            sp.wait_ge(idx_made, 1)

            def edges(slot):
                s = slot.step(0)
                if s:
                    wait(sp, turned, s.j - RE + 1)
                    if s.known and s.j < EARLY:
                        pass
                    else:
                        sp.dma_start(src_slot[:, s.slot, :, :], src_idx[:, bass.ds(s.j * G, G), :]).then_inc(src_here[s.slot], 16)
                    if s.known and s.j < EARLY:
                        pass
                    elif s.known and s.j == NI - 1:
                        e0 = HALF + s.j * GROUP
                        full = (E - e0) // P
                        more = E - e0 - full * P
                        sp.dma_start(e_sum[:, s.slot, :, 0, :], edge_rows(edge_attr, 0, s.j)).then_inc(attr_here[s.slot], 16)
                        sp.dma_start(e_sum[:, s.slot, 0:full, 1, :], edge_attr[e0:e0 + full * P, :].rearrange(
                            "(k p) c -> p k c", p=P)).then_inc(attr_here[s.slot], 16)
                        sp.dma_start(e_sum[0:more, s.slot, full, 1, :], edge_attr[e0 + full * P:E, :]).then_inc(
                            attr_here[s.slot], 16)
                    else:
                        for half in range(2):
                            sp.dma_start(e_sum[:, s.slot, :, half, :], edge_rows(edge_attr, half, s.j)).then_inc(
                                attr_here[s.slot], 16)
                s = slot.step(-7)
                if s:
                    wait(sp, rows_made, s.j + 1)
                    for half in range(2):
                        sp.dma_start(edge_rows(seg_rows, half, s.j), row_out[:, s.slot % 2, :, half, :]).then_inc(
                            rows_stored[s.slot], 16)

            pipeline(sp, edges, NI, RE, 0, 7)

            sp.wait_ge(p_dve, 11)

            def nodes(slot):
                s = slot.step(0)
                if s:
                    wait(sp, o_summed, s.j - 3)
                    sp.dma_start(last_slot[:, s.slot % 4, :], last_edge[:, bass.ds(s.j, 1), :].rearrange(
                        "p b k -> p (b k)")).then_inc(last_here[s.slot], 16)
                    wait(sp, z_made, s.j - R + 1)
                    if s.known and s.j == NB - 1:
                        sp.dma_start(x_in[0:tail_nodes, s.slot, :, :], x[s.j * GROUP:N, :].rearrange(
                            "(p k) c -> p k c", k=G)).then_inc(x_here[s.slot], 16)
                    else:
                        sp.dma_start(x_in[:, s.slot, :, :], node_rows(x, s.j)).then_inc(x_here[s.slot], 16)
                s = slot.step(-10)
                if s:
                    wait(sp, normed, s.j + 1)
                    if s.known and s.j == NB - 1:
                        sp.dma_start(out[s.j * GROUP:N, :].rearrange("(p k) c -> p k c", k=G),
                                     res[0:tail_nodes, s.slot % 4, :, :]).then_inc(out_stored[s.slot], 16)
                    else:
                        sp.dma_start(node_rows(out, s.j), res[:, s.slot % 4, :, :]).then_inc(out_stored[s.slot], 16)

            pipeline(sp, nodes, NB, R, 0, 10)
            for i in range(R):
                sp.wait_ge(out_stored[i], 16 * len(range(i, NB, R)))

        @block.gpsimd
        def _(pool):
            nc.gpsimd.memset(raw[:, 0, :, :], 0).then_inc(ramps_made, 1)
            nc.gpsimd.memset(raw[:, 1, :, :], 65535).then_inc(ramps_made, 1)
            nc.gpsimd.memset(raw[:, 2, :, :], -1).then_inc(ramps_made, 1)
            pool.wait_ge(ramps_made, 3)
            nc.gpsimd.memset(zero_row[:, :], 0.0).then_inc(pads_set, 1)
            nc.gpsimd.iota(ramp[:, :], [[1, P]], base=0, channel_multiplier=-1,
                           allow_small_or_imprecise_dtypes=True).then_inc(ramps_made, 1)
            nc.gpsimd.iota(node_ramp[:, :], [[1, P]], base=0, channel_multiplier=0,
                           allow_small_or_imprecise_dtypes=True).then_inc(ramps_made, 1)
            nc.gpsimd.iota(col_ramp[:, :], [[1, NC]], base=-(NC // 2), channel_multiplier=0,
                           allow_small_or_imprecise_dtypes=True).then_inc(ramps_made, 1)
            pool.wait_ge(pads_set, 1)
            nc.gpsimd.memset(snap[:, :, :], 0.0).then_inc(zero_set, 1)

            def edges(slot):
                s = slot.step(0)
                if s:
                    pool.wait_ge(src_here[s.slot], 16 * s.turn + (32 if s.slot < EARLY else 16))
                    pool.sem_inc(gathers_open, 1)
                    for k in range(G):
                        for half in range(2):
                            nc.gpsimd.indirect_dma_start(
                                out=x_src[:, s.slot, k, half, :], out_offset=None, in_=x,
                                in_offset=bass.IndirectOffsetOnAxis(ap=src_slot[:, s.slot, k, half:half + 1], axis=0),
                            ).then_inc(gathered[s.slot], 16)

            pipeline(pool, edges, NI, RE, 0, 0)

            all_rows_stored(pool)
            pool.wait_ge(merged_stored, 32)

            def nodes(slot):
                s = slot.step(0)
                if s:
                    pool.wait_ge(last_here[s.slot], 16 * s.turn + 16)
                    wait(pool, o_summed, s.j - 3)
                    pool.sem_inc(gathers_open, 1)
                    for k in range(G):
                        nc.gpsimd.indirect_dma_start(
                            out=agg[:, s.slot % 4, k, :], out_offset=None, in_=seg_rows,
                            in_offset=bass.IndirectOffsetOnAxis(ap=last_slot[:, s.slot % 4, k:k + 1], axis=0),
                        ).then_inc(agg_here[s.slot], 16)

            pipeline(pool, nodes, NB, R, 0, 0)

        @block.vector
        def _(dve):
            v = nc.vector
            steps = [0]

            def then(ins, last=True):
                steps[0] += 1
                ins.then_inc(prep, 1)
                if last:
                    dve.wait_ge(prep, steps[0])

            dve.wait_ge(ramps_made, 6)
            then(v.memset(ones[:, :], 1.0), last=False)
            then(v.memset(mean_w[:, :], 1.0 / P), last=False)
            then(v.memset(eps_col[:, 0:1], EPS), last=False)
            then(v.memset(eps_col[:, 1:2], LN_EPS), last=False)
            then(v.memset(one_col[:, :], 1.0), last=False)
            then(v.memset(state[:, 0, 0, 0:1], 0.0), last=False)
            then(v.tensor_scalar(ident[:, :], ramp[:, :], 0.0, None, ALU.is_equal), last=False)
            then(v.tensor_scalar(before_w[:, :], ramp[:, :], 0.0, None, ALU.is_gt), last=False)
            then(v.tensor_copy(node_ids[:, :], node_ramp[:, :]), last=False)
            then(v.tensor_copy(col_ids[:, :], col_ramp[:, :]))
            for a in range(2):
                for h in range(2):
                    then(v.tensor_copy(pick[:, a, h * C:(h + 1) * C],
                                       ident[0:4, 2 * a + h:2 * a + h + 1].broadcast_to((4, C))), last=False)
            then(v.tensor_scalar(minus_ident[:, :], ident[:, :], -1.0, None, ALU.mult), last=False)
            then(v.tensor_scalar(center[:, :], ident[:, :], -1.0 / P, None, ALU.add), last=False)
            dve.wait_ge(prep, steps[0])
            dve.wait_ge(tiles_loaded, 176)
            v.tensor_copy(rawf[:, :, :, :], raw[:, :, :, :]).then_inc(consts_made, 1)
            dve.wait_ge(consts_made, 1)
            v.tensor_tensor(same_rows[:, 0], rawf[:, 1], rawf[:, 2], ALU.is_equal).then_inc(masks_made, 1)
            dve.wait_ge(masks_made, 1)
            v.memset(same_rows[0:1, 0, 2, 0:1], 0.0).then_inc(mask_cut, 1)
            dve.wait_ge(mask_cut, 1)
            v.tensor_scalar(same_rows[:, 1], same_rows[:, 0], -1.0, NEVER, ALU.add, ALU.mult).then_inc(masks_made, 1)
            dve.wait_ge(idx_turned, 1)

            def by_tile(t):
                return t[:, :, :].rearrange("p (g t) h -> p h g t", g=2)

            def idx(a):
                return idx_ps[:, a, :, :].rearrange("p (h g) t -> p h g t", h=2)

            for h in range(2):
                then(v.tensor_copy(by_tile(src_idx)[:, h], idx(0)[:, h]), last=False)
                then(v.tensor_copy(by_tile(dst_f)[:, h], idx(1)[:, h]), last=False)
                then(v.tensor_copy(by_tile(dst_i)[:, h], idx(1)[:, h]), last=h == 1)
            then(v.tensor_scalar(int_a[:, :, :], dst_i[:, :, :], 2, P - 1, ALU.arith_shift_right, ALU.bitwise_and))
            then(v.tensor_scalar(minus_p[:, :, :], int_a[:, :, :], -1.0, None, ALU.mult))
            then(v.tensor_scalar(int_a[:, :, :], dst_i[:, :, :], 9, None, ALU.arith_shift_right))
            then(v.tensor_scalar(dst_c[:, :, :], int_a[:, :, :], float(G), float(-(NC // 2)), ALU.mult, ALU.add))
            then(v.tensor_scalar(int_a[:, :, :], dst_i[:, :, :], G - 1, None, ALU.bitwise_and))
            then(v.tensor_tensor(dst_c[:, :, :], dst_c[:, :, :], int_a[:, :, :], ALU.add))
            dve.wait_ge(weights_loaded, 16 * 12)
            then(v.tensor_copy(mid_f[:, :], mid_i[:, :]))
            then(v.tensor_scalar(in_run[:, :], dst_f[:, :, 1], mid_f[:, 1:2], None, ALU.is_equal))
            v.tensor_reduce(mid_cnt[:, 0:1], in_run[:, :], AX_X, ALU.add).then_inc(idx_made, 1)
            dve.wait_ge(idx_made, 1)
            then(v.tensor_tensor(mid_cnt[:, 1:2], mid_f[:, 0:1], mid_f[:, 1:2], ALU.is_equal))
            dve.wait_ge(mid_counted, 1)
            then(v.tensor_scalar(mid_cnt[:, 2:3], small_ps[:, 0:1], -1.0, None, ALU.add))
            then(v.tensor_copy(mid_int[:, 0:1], mid_cnt[:, 2:3]))
            then(v.tensor_scalar(mid_int[:, 1:2], mid_int[:, 0:1], GROUP - 1, None, ALU.bitwise_and))
            then(v.tensor_scalar(mid_int[:, 2:3], mid_int[:, 0:1], GROUP.bit_length() - 1, None, ALU.arith_shift_right))
            then(v.tensor_scalar(mid_cnt[:, 3:4], mid_cnt[:, 2:3], float(MID - ZERO_ROW - NO_ROW), None, ALU.add))
            then(v.tensor_tensor(mid_cnt[:, 3:4], mid_cnt[:, 3:4], mid_cnt[:, 1:2], ALU.mult))
            then(v.tensor_scalar(mid_cnt[:, 3:4], mid_cnt[:, 3:4], float(NO_ROW), None, ALU.add))
            then(v.tensor_scalar(mid_cnt[:, 4:5], mid_cnt[:, 3:4], -1.0, float(MERGED_ROW - ZERO_ROW),
                                 ALU.mult, ALU.add), last=False)
            dve.wait_ge(w_turned, 1)
            then(v.memset(w1_t[:, :, :], 0.0))
            for half in range(2):
                rows = slice(half * C, half * C + C)
                then(v.tensor_copy(w1_t[rows, half, :], w_ps[rows, 0:P]), last=False)
            then(v.tensor_copy(w2_t[:, :], w_ps[:, P:P + C]), last=False)
            then(v.memset(ones_b[:, :], 1.0), last=False)
            then(v.tensor_copy(b2_part[:, 0], b2_row[:, :, :]))
            then(v.tensor_tensor(b2_rest[:, 0], b2_row[:, :, :], b2_part[:, 0], ALU.subtract))
            then(v.tensor_copy(b2_part[:, 1], b2_rest[:, 0]))
            then(v.tensor_tensor(b2_rest[:, 1], b2_rest[:, 0], b2_part[:, 1], ALU.subtract))
            then(v.tensor_copy(b2_part[:, 2], b2_rest[:, 1]))
            v.tensor_copy(b1_c[:, :], w_ps[:, P + C:P + C + 1]).then_inc(w_made, 1)
            column = dve.value_load(mid_int[0:1, 1:2], min_val=0, max_val=GROUP - 1)
            turn_of = dve.value_load(mid_int[0:1, 2:3], min_val=0, max_val=NI - 1)

            def count_up_to():
                dve.wait_ge(counted, NI)
                v.tensor_copy(count[:, :, :], count_ps.rearrange("p (b k) -> p b k", k=G)).then_inc(p_dve, 1)
                dve.wait_ge(p_dve, 1)
                v.tensor_copy(upto[:, :, 0], count[:, :, 0]).then_inc(p_dve, 1)
                for k in range(1, G):
                    dve.wait_ge(p_dve, k + 1)
                    v.tensor_tensor(upto[:, :, k], upto[:, :, k - 1], count[:, :, k], ALU.add).then_inc(p_dve, 1)

            def find_block_starts():
                dve.wait_ge(p_pe, 1)
                v.tensor_copy(block_n[:, :], small_ps[:, 256:256 + NB]).then_inc(p_dve, 1)
                dve.wait_ge(p_dve, 6)
                v.tensor_tensor_scan(block_end[:, :], ones[:, 0:NB], block_n[:, :], 0.0, ALU.mult, ALU.add).then_inc(p_dve, 1)
                dve.wait_ge(p_dve, 7)
                v.tensor_tensor(block_0[:, :], block_end[:, :], block_n[:, :], ALU.subtract).then_inc(p_dve, 1)
                dve.wait_ge(p_dve, 8)
                v.tensor_tensor(block_0[:, :], block_0[:, :], small_ps[:, 128:128 + NB], ALU.add).then_inc(p_dve, 1)
                v.tensor_scalar(some[:, :, :], count[:, :, :], 0.0, None, ALU.is_gt).then_inc(p_dve, 1)

            def find_last_edges():
                dve.wait_ge(p_dve, 10)
                v.tensor_tensor(upto[:, :, :], upto[:, :, :], block_0[:, :].rearrange("p (b a) -> p b a", a=1).broadcast_to(
                    (P, NB, G)), ALU.add).then_inc(mid_made, 1)
                dve.wait_ge(mid_made, 1)
                v.scalar_tensor_tensor(upto[:, :, :], upto[:, :, :], float(-1 - ZERO_ROW), some[:, :, :],
                                       ALU.add, ALU.mult).then_inc(mid_made, 1)
                dve.wait_ge(mid_made, 2)
                v.tensor_scalar(cut_row[:, :, :], upto[:, :, :], mid_cnt[:, 3:4], None, ALU.is_equal).then_inc(mid_made, 1)
                dve.wait_ge(mid_made, 3)
                v.scalar_tensor_tensor(upto[:, :, :], cut_row[:, :, :], mid_cnt[:, 4:5], upto[:, :, :],
                                       ALU.mult, ALU.add).then_inc(mid_made, 1)
                dve.wait_ge(mid_made, 4)
                v.tensor_scalar(last_edge[:, :, :], upto[:, :, :], float(ZERO_ROW), None, ALU.add).then_inc(p_dve, 1)

            def edges(slot):
                s = slot.step(0)
                if s:
                    dve.wait_ge(turned, s.j + 1)
                    dve.wait_ge(same_copied, s.j + 1)
                    wait(dve, carried, s.j)
                    wait(dve, drop_made, s.j - 1)
                    wait(dve, snapped, s.j - 1)
                    v.tensor_tensor_scan(state[:, s.slot % 2, 0, 1:], same_bc[:, s.slot % 2, :], msg_ps[:, s.slot % 2, :],
                                         state[:, s.slot % 2, 0, 0:1], ALU.mult, ALU.max).then_inc(maxed, 1)
                if s and s.known and s.j == NI - 1:
                    find_last_edges()
                r = slot.step(-1)
                if r:
                    dve.wait_ge(e_made, r.j + 1)
                    v.scalar_tensor_tensor(e_msg[:, r.slot % 2, :], msg_ps[:, r.slot % 2, :], 0.0, e_exp[:, r.slot % 2, :],
                                           ALU.max, ALU.mult).then_inc(weighed, 1)
                    dve.wait_ge(c_made, r.j + 1)
                    wait(dve, log_made, r.j - 1)
                    first = r.known and r.j == 0
                    if not first:
                        dve.wait_ge(d_made, r.j)
                    v.tensor_tensor_scan(state[:, r.slot % 2, 1, 1:], c_exp[:, r.slot % 2, :], e_exp[:, r.slot % 2, :],
                                         0.0 if first else state[:, 1 - r.slot % 2, 1, GROUP:GROUP + 1],
                                         ALU.mult, ALU.add).then_inc(d_made, 1)
                if s and not (s.known and s.j == NI - 1):
                    dve.wait_ge(maxed, s.j + 1)
                    wait(dve, drop_made, s.j)
                    v.tensor_copy(state[:, 1 - s.slot % 2, 0, 0:1], state[:, s.slot % 2, 0, GROUP:GROUP + 1]).then_inc(carried, 1)
                if s:
                    dve.wait_ge(maxed, s.j + 1)
                    wait(dve, e_made, s.j - 1)
                    v.scalar_tensor_tensor(below[:, s.slot % 2, :], msg_ps[:, s.slot % 2, :], 0.0, state[:, s.slot % 2, 0, 1:],
                                           ALU.max, ALU.subtract).then_inc(below_made, 1)
                if r:
                    dve.wait_ge(weighed, r.j + 1)
                    if not first:
                        dve.wait_ge(a_made, r.j)
                    v.tensor_tensor_scan(state[:, r.slot % 2, 2, 1:], c_exp[:, r.slot % 2, :], e_msg[:, r.slot % 2, :],
                                         0.0 if first else state[:, 1 - r.slot % 2, 2, GROUP:GROUP + 1],
                                         ALU.mult, ALU.add).then_inc(a_made, 1)
                q = slot.step(-2)
                if q and q.known and q.j == NI - 1:
                    dve.wait_ge(snapped, NI)
                    v.tensor_copy(mrg[:, 0:3], snap[:, bass.ds(turn_of, 1), :].rearrange("p a q -> p (a q)")).then_inc(m_dve, 1)
                if q:
                    dve.wait_ge(inv_made, q.j + 1)
                    wait(dve, turned_back, q.j - 1)
                    v.tensor_tensor(quot[:, q.slot % 2, :], state[:, q.slot % 2, 2, 1:], log_d[:, q.slot % 2, :],
                                    ALU.mult).then_inc(divided, 1)
                if r:
                    dve.wait_ge(a_made, r.j + 1)
                    dve.wait_ge(d_made, r.j + 1)
                    v.tensor_copy(snap[C:P, bass.ds(r.j, 1), :].rearrange("p a q -> p (a q)"),
                                  state[C:P, r.slot % 2, :, bass.ds(column + 1, 1)].rearrange("p q a -> p (q a)")).then_inc(snapped, 1)
                n = slot.step(1)
                if n and n.known and n.j == NI - 1:
                    count_up_to()
                    find_block_starts()
                if n:
                    dve.wait_ge(gathered[n.slot], 128 * n.turn + 128)
                    dve.wait_ge(attr_here[n.slot], 32 * n.turn + (48 if n.known and n.j == NI - 1 else 32))
                    v.tensor_tensor(e_sum[:, n.slot], e_sum[:, n.slot], x_src[:, n.slot], ALU.add).then_inc(e_summed, 1)
                h = slot.step(3)
                if h:
                    wait(dve, counted, h.j - 1)
                    for k in range(G):
                        for half in range(2):
                            ins = v.tensor_scalar(hot_c[:, h.slot % 2, 2 * k + half, :], col_ids[:, :],
                                                  dst_c[:, bass.ds(h.j * G + k, 1), half], None, ALU.is_equal)
                    ins.then_inc(hot_c_made, 1)

            dve.wait_ge(zero_set, 1)
            pipeline(dve, edges, NI, RE, 3, 2)

            L = (NI - 1) % 2
            dve.wait_ge(m_pe, 1)
            v.tensor_copy(mrg[0:C, 3:6], small_ps[0:C, 8:11]).then_inc(m_dve, 1)
            dve.wait_ge(m_dve, 2)
            v.tensor_tensor(mrg[0:C, 6:7], mrg[0:C, 3:4], state[0:C, L, 0, GROUP:GROUP + 1], ALU.max).then_inc(m_dve, 1)
            dve.wait_ge(m_dve, 3)
            v.tensor_tensor(mrg[0:C, 7:8], state[0:C, L, 0, GROUP:GROUP + 1], mrg[0:C, 6:7], ALU.subtract).then_inc(m_dve, 1)
            v.tensor_tensor(mrg[0:C, 8:9], mrg[0:C, 3:4], mrg[0:C, 6:7], ALU.subtract).then_inc(m_dve, 1)
            dve.wait_ge(m_act, 1)
            v.tensor_scalar(mrg[0:C, 11:13], state[0:C, L, 1:3, GROUP], mrg[0:C, 9:10], None, ALU.mult).then_inc(m_dve, 1)
            dve.wait_ge(m_dve, 6)
            v.scalar_tensor_tensor(mrg[0:C, 13:15], mrg[0:C, 4:6], mrg[0:C, 10:11], mrg[0:C, 11:13],
                                   ALU.mult, ALU.add).then_inc(m_dve, 1)
            dve.wait_ge(m_dve, 7)
            v.reciprocal(mrg[0:C, 12:13], mrg[0:C, 13:14]).then_inc(m_dve, 1)
            dve.wait_ge(m_dve, 8)
            v.tensor_scalar(mrg[0:C, 15:16], mrg[0:C, 14:15], mrg[0:C, 12:13], EPS, ALU.mult, ALU.add).then_inc(m_dve, 1)

            def nodes(slot):
                s = slot.step(-3)
                if s:
                    dve.wait_ge(hinv_made, s.j + 1)
                    wait(dve, y_made, s.j - 1)
                    v.scalar_tensor_tensor(h_n[:, s.slot % 2].rearrange("p r q n -> p r (q n)"), h_ps[:, s.slot % 4],
                                           b1_c[:, 0:1], inv[:, s.slot % 2], ALU.add, ALU.mult).then_inc(h_scaled, 1)
                s = slot.step(0)
                if s:
                    dve.wait_ge(agg_here[s.slot], 64 * s.turn + 64)
                    dve.wait_ge(x_here[s.slot], 16 * s.turn + 16)
                    wait(dve, o_turned, s.j - 1)
                    v.tensor_tensor(o_sum[:, s.slot % 2], agg[:, s.slot % 4], x_in[:, s.slot], ALU.add).then_inc(o_summed, 1)
                s = slot.step(-4)
                if s:
                    dve.wait_ge(y_made, s.j + 1)
                    v.tensor_tensor(z[:, s.slot % 4], y_ps[:, s.slot % 2].rearrange("p (k c) -> p k c", k=G),
                                    x_in[:, s.slot], ALU.add).then_inc(z_made, 1)
                    dve.wait_ge(z_made, s.j + 1)
                    v.tensor_reduce(z_sum[:, s.slot % 2, :], z[:, s.slot % 4], AX_X, ALU.add).then_inc(z_summed, 1)
                    dve.wait_ge(z_summed, s.j + 1)
                    v.scalar_tensor_tensor(z[:, s.slot % 4], z_sum[:, s.slot % 2, :].rearrange(
                        "p (k a) -> p k a", a=1).broadcast_to((P, G, C)), -1.0 / C, z[:, s.slot % 4],
                        ALU.mult, ALU.add).then_inc(z_centered, 1)
                s = slot.step(-5)
                if s:
                    dve.wait_ge(z_squared, s.j + 1)
                    wait(dve, zlog_made, s.j - 1)
                    v.tensor_reduce(z_var[:, s.slot % 2, :], z_sq[:, s.slot % 2], AX_X, ALU.add).then_inc(zvar_made, 1)
                s = slot.step(-6)
                if s:
                    dve.wait_ge(zinv_made, s.j + 1)
                    t = Step(s.turn, s.slot - 4, R)
                    if not t.known or t.j >= 0:
                        dve.wait_ge(out_stored[t.slot], 16 * t.turn + 16)
                    v.tensor_tensor(res[:, s.slot % 4], z[:, s.slot % 4], z_inv[:, s.slot % 2, :].rearrange(
                        "p (k a) -> p k a", a=1).broadcast_to((P, G, C)), ALU.mult).then_inc(normed, 1)

            pipeline(dve, nodes, NB, R, 0, 6, back=6 + 4)

        @block.tensor
        def _(pe):
            t = nc.tensor
            pe.wait_ge(consts_made, 1)
            for a in range(2):
                for g in range(4):
                    ins = t.transpose(idx_ps[:, a, g, :], rawf[0:TG, a, g, :], ident[0:TG, 0:TG])
            ins.then_inc(idx_turned, 1)
            pe.wait_ge(weights_loaded, 16 * 12)
            t.matmul(w_ps[:, 0:P], w1_in[:, :, :].rearrange("p a c -> p (a c)"),
                     center[:, :], start=True, stop=True)
            t.matmul(w_ps[:, P + C:P + C + 1], center[:, :], vecs[:, 0:1], start=True, stop=True)
            t.transpose(w_ps[:, P:P + C], w2_in[:, :], ident[0:C, 0:C]).then_inc(w_turned, 1)
            pe.wait_ge(idx_made, 1)
            t.matmul(small_ps[:, 0:1], ones[:, :], mid_cnt[:, 0:1], start=True, stop=True).then_inc(mid_counted, 1)
            pe.wait_ge(w_made, 1)
            pe.wait_ge(masks_here, 16)
            def edges(slot):
                s = slot.step(1)
                if s:
                    wait(pe, same_copied, s.j)
                    t.matmul(same_ps, pick[:, 0, :], masks[:, bass.ds(s.j * GROUP, GROUP)],
                             start=True, stop=True).then_inc(same_spread, 1)
                s = slot.step(0)
                if s:
                    pe.wait_ge(maxed, s.j + 1)
                    wait(pe, carried, s.j)
                    wait(pe, c_made, s.j - 1)
                    t.matmul(drop_ps[:, s.slot % 2, :], ident[:, :], state[:, s.slot % 2, 0, 0:GROUP], start=True, stop=False,
                             skip_group_check=True)
                    t.matmul(drop_ps[:, s.slot % 2, :], minus_ident[:, :], state[:, s.slot % 2, 0, 1:], start=False, stop=False,
                             skip_group_check=True)
                    t.matmul(drop_ps[:, s.slot % 2, :], pick[:, 1, :], masks[:, bass.ds(s.j * GROUP, GROUP)],
                             start=False, stop=True, skip_group_check=True).then_inc(drop_made, 1)
                q = slot.step(-2)
                if q and q.known and q.j == NI - 1:
                    pe.wait_ge(m_dve, 1)
                    t.matmul(small_ps[0:C, 8:11], ident[:, C:P], mrg[:, 0:3], start=True, stop=True).then_inc(m_pe, 1)
                if q:
                    pe.wait_ge(divided, q.j + 1)
                    wait(pe, rows_made, q.j)
                    for k in range(G):
                        ins = t.transpose(back_ps[:, k * P:(k + 1) * P], quot[:, q.slot % 2, k * P:(k + 1) * P], ident[:, :])
                    ins.then_inc(turned_back, 1)
                h = slot.step(2)
                if h:
                    pe.wait_ge(hot_p_made, h.j + 1)
                    pe.wait_ge(hot_c_made, h.j + 1)
                    for n in range(2 * G):
                        ins = t.matmul(count_ps, hot_p[:, h.slot % 2, n, :], hot_c[:, h.slot % 2, n, :],
                                       start=(h.known and h.j == 0 and n == 0),
                                       stop=(h.known and h.j == NI - 1 and n == 2 * G - 1), skip_group_check=True)
                    ins.then_inc(counted, 1)
                s = slot.step(1)
                if s and s.known and s.j == NI - 1:
                    pe.wait_ge(p_dve, 5)
                    t.matmul(small_ps[:, 128:128 + NB], before_w[:, :], upto[:, :, G - 1], start=True, stop=True)
                    t.matmul(small_ps[:, 256:256 + NB], ones[:, :], upto[:, :, G - 1], start=True, stop=True).then_inc(p_pe, 1)
                if s:
                    pe.wait_ge(e_summed, s.j + 1)
                    wait(pe, weighed, s.j - 1)
                    for k in range(G):
                        ins = t.transpose(msg_ps[:, s.slot % 2, k * P:(k + 1) * P],
                                          e_sum[:, s.slot, k].rearrange("p h c -> p (h c)"), ident[:, :])
                    ins.then_inc(turned, 1)

            pipeline(pe, edges, NI, RE, 2, 2)

            pe.wait_ge(m_dve, 2)
            pe.wait_ge(p_dve, 9)
            pe.wait_ge(rows_made, NI)
            pe.wait_ge(c_made, NI)
            pe.wait_ge(weighed, NI)

            def nodes(slot):
                s = slot.step(-4)
                if s:
                    wait(pe, z_made, s.j - 1)
                    for part in range(3):
                        t.matmul(y_ps[:, s.slot % 2], ones_b[:, :], b2_part[:, part].rearrange("p k c -> p (k c)"),
                                 start=(part == 0), stop=False, skip_group_check=True)
                    pe.wait_ge(h_relu, s.j + 1)
                    for k in range(G):
                        ins = t.matmul(y_ps[:, s.slot % 2, k * C:(k + 1) * C], h_n[:, s.slot % 2, k % 2, k // 2, :],
                                       w2_t[:, :], start=False, stop=(k == G - 1), skip_group_check=True)
                    ins.then_inc(y_made, 1)
                s = slot.step(-2)
                if s:
                    pe.wait_ge(sq_made, s.j + 1)
                    wait(pe, hlog_made, s.j)
                    t.matmul(var_ps, mean_w[:, :], sq[:, s.slot % 2].rearrange("p r n -> p (r n)"),
                             start=True, stop=True).then_inc(var_made, 1)
                s = slot.step(-1)
                if s:
                    pe.wait_ge(o_copied, s.j + 1)
                    wait(pe, h_scaled, s.j - 3)
                    for half in range(2):
                        ins = t.matmul(h_ps[:, s.slot % 4, half, :], w1_t[:, half, :],
                                       o_t[:, s.slot % 2].rearrange("p q n -> p (q n)"), start=True, stop=True)
                    ins.then_inc(h_made, 1)
                s = slot.step(0)
                if s:
                    pe.wait_ge(o_summed, s.j + 1)
                    wait(pe, o_copied, s.j)
                    for q in range(2):
                        ins = t.transpose(ot_ps[:, q * P:(q + 1) * P],
                                          o_sum[:, s.slot % 2, 2 * q:2 * q + 2, :].rearrange("p k c -> p (k c)"), ident[:, :])
                    ins.then_inc(o_turned, 1)

            pipeline(pe, nodes, NB, R, 0, 6)

        @block.scalar
        def _(act):
            a = nc.scalar
            a.preload_act_table_set("natural_log_exp_and_others")
            for j in range(EARLY):
                if j:
                    early(act, j)
                for half in range(2):
                    act.dma_start(e_sum[:, j, :, half, :], edge_rows(edge_attr, half, j)).then_inc(attr_here[j], 16)
            for c in range(2):
                act.dma_start(mid_i[:, c:c + 1], dst[MID - 1 + c:MID + c].rearrange(
                    "(a b) -> a b", a=1).broadcast_to((P, 1))).then_inc(weights_loaded, 16)
            act.dma_start(w1_in[:, 0, :], W1).then_inc(weights_loaded, 16)
            act.dma_start(w1_in[:, 1, :], W1).then_inc(weights_loaded, 16)
            act.dma_start(w2_in[:, :], W2).then_inc(weights_loaded, 16)
            for c, table in enumerate((b1, g1, be1)):
                act.dma_start(vecs[:, c:c + 1], table.rearrange("(p a) -> p a", a=1)).then_inc(weights_loaded, 16)
            for k in range(G):
                act.dma_start(b2_row[:, k, :], b2.rearrange("(a c) -> a c", a=1)).then_inc(weights_loaded, 16)
            act.wait_ge(idx_made, 1)

            def stored_before(s, back):
                t = Step(s.turn, s.slot - back, RE)
                if not t.known or t.j >= 0:
                    act.wait_ge(rows_stored[t.slot], 32 * t.turn + 32)

            def edges(slot):
                s = slot.step(1)
                if s:
                    act.wait_ge(same_spread, s.j + 1)
                    wait(act, maxed, s.j - 1)
                    a.activation(same_bc[:, s.slot % 2, :], same_ps, ACT.Copy).then_inc(same_copied, 1)
                s = slot.step(0)
                if s:
                    act.wait_ge(drop_made, s.j + 1)
                    wait(act, a_made, s.j - 1)
                    a.activation(c_exp[:, s.slot % 2, :], drop_ps[:, s.slot % 2, :], ACT.Exp).then_inc(c_made, 1)
                    act.wait_ge(below_made, s.j + 1)
                    a.activation(e_exp[:, s.slot % 2, :], below[:, s.slot % 2, :], ACT.Exp).then_inc(e_made, 1)
                r = slot.step(-1)
                if r:
                    act.wait_ge(d_made, r.j + 1)
                    wait(act, divided, r.j - 1)
                    a.activation(log_d[:, r.slot % 2, :], state[:, r.slot % 2, 1, 1:], ACT.Ln).then_inc(log_made, 1)
                    act.wait_ge(log_made, r.j + 1)
                    a.activation(log_d[:, r.slot % 2, :], log_d[:, r.slot % 2, :], ACT.Exp, scale=-1.0).then_inc(inv_made, 1)
                q = slot.step(-2)
                if q and q.known and q.j == NI - 1:
                    act.wait_ge(m_dve, 5)
                    a.activation(mrg[0:C, 9:11], mrg[0:C, 7:9], ACT.Exp).then_inc(m_act, 1)
                if q:
                    act.wait_ge(turned_back, q.j + 1)
                    stored_before(q, 2)
                    a.activation(row_out[:, q.slot % 2].rearrange("p k h c -> p (k h c)"), back_ps, ACT.Identity,
                                 bias=eps_col[:, 0:1]).then_inc(rows_made, 1)
                h = slot.step(3)
                if h:
                    wait(act, hot_p_made, h.j)
                    for k in range(G):
                        for half in range(2):
                            ins = a.activation(off_p[:, 2 * k + half, :], node_ids[:, :], ACT.Abs,
                                               bias=minus_p[:, bass.ds(h.j * G + k, 1), half])
                    ins.then_inc(off_made, 1)
                    act.wait_ge(off_made, h.j + 1)
                    wait(act, counted, h.j - 1)
                    a.activation(hot_p[:, h.slot % 2], off_p[:, :, :], ACT.Relu, scale=-1.0,
                                 bias=one_col[:, 0:1]).then_inc(hot_p_made, 1)

            pipeline(act, edges, NI, RE, 3, 2)
            act.wait_ge(m_dve, 9)
            act.dma_start(seg_rows[MERGED_ROW:MERGED_ROW + 1, :].rearrange("a c -> c a"), mrg[0:C, 15:16],
                          allow_slow_non_contiguous=True).then_inc(merged_stored, 16)

            def nodes(slot):
                s = slot.step(-3)
                if s:
                    act.wait_ge(h_scaled, s.j + 1)
                    hv = h_n[:, s.slot % 2].rearrange("p r q n -> p (r q n)")
                    a.activation(hv, hv, ACT.Relu, bias=vecs[:, 2:3], scale=vecs[:, 1:2]).then_inc(h_relu, 1)
                s = slot.step(-5)
                if s:
                    act.wait_ge(z_centered, s.j + 1)
                    wait(act, zvar_made, s.j - 1)
                    a.activation(z_sq[:, s.slot % 2], z[:, s.slot % 4], ACT.Square).then_inc(z_squared, 1)
                s = slot.step(-2)
                if s:
                    act.wait_ge(var_made, s.j + 1)
                    wait(act, h_scaled, s.j - 1)
                    iv = inv[:, s.slot % 2].rearrange("p r n -> p (r n)")
                    a.activation(iv, var_ps, ACT.Ln, bias=eps_col[:, 1:2]).then_inc(hlog_made, 1)
                    act.wait_ge(hlog_made, s.j + 1)
                    a.activation(iv, iv, ACT.Exp, scale=-0.5).then_inc(hinv_made, 1)
                s = slot.step(-1)
                if s:
                    act.wait_ge(h_made, s.j + 1)
                    wait(act, var_made, s.j - 1)
                    a.activation(sq[:, s.slot % 2], h_ps[:, s.slot % 4], ACT.Square, bias=b1_c[:, 0:1]).then_inc(sq_made, 1)
                s = slot.step(0)
                if s:
                    act.wait_ge(o_turned, s.j + 1)
                    wait(act, h_made, s.j - 1)
                    a.activation(o_t[:, s.slot % 2].rearrange("p q n -> p (q n)"), ot_ps, ACT.Copy).then_inc(o_copied, 1)
                s = slot.step(-5)
                if s:
                    act.wait_ge(zvar_made, s.j + 1)
                    wait(act, normed, s.j - 1)
                    a.activation(z_log[:, s.slot % 2, :], z_var[:, s.slot % 2, :], ACT.Ln, bias=eps_col[:, 1:2],
                                 scale=1.0 / C).then_inc(zlog_made, 1)
                    act.wait_ge(zlog_made, s.j + 1)
                    a.activation(z_inv[:, s.slot % 2, :], z_log[:, s.slot % 2, :], ACT.Exp, scale=-0.5).then_inc(zinv_made, 1)

            pipeline(act, nodes, NB, R, 0, 6)


_INS = ['x', 'src', 'dst', 'edge_attr_64', 'L0_gnn_W1', 'L0_gnn_b1', 'L0_gnn_g1', 'L0_gnn_be1', 'L0_gnn_W2', 'L0_gnn_b2']
_OUTS = [((50000, 64), 'float32')]


def kernel(**inputs):
    import numpy as _np
    import concourse.bacc as _bacc
    from concourse import mybir as _mybir
    from concourse.bass_utils import run_bass_kernel_spmd as _run

    nc = _bacc.Bacc("TRN2", target_bir_lowering=False, num_devices=1)
    arrays, args = {}, []
    for name in _INS:
        a = _np.ascontiguousarray(inputs[name])
        arrays[f"in_{name}_dram"] = a
        args.append(nc.dram_tensor(f"in_{name}_dram", a.shape, _mybir.dt.from_np(a.dtype), kind="ExternalInput").ap())
    for i, (shape, dtype) in enumerate(_OUTS):
        dt = _mybir.dt.from_np(_np.dtype(dtype))
        args.append(nc.dram_tensor(f"out_{i}_dram", shape, dt, kind="ExternalOutput").ap())
    gnn_resnorm(nc, *args)
    r = _run(nc, [arrays], core_ids=[0])
    got = tuple(r.results[0][f"out_{i}_dram"] for i in range(len(_OUTS)))
    return got[0]
```
